# Optimizing a Trainium2 kernel written in Bass

```python
import numpy as np
import jax
import jax.numpy as jnp

def _softmax(x, axis=-1):
    return jax.nn.softmax(x, axis=axis)

def _gelu(x):
    return jax.nn.gelu(x, approximate=True)

def _silu(x):
    return jax.nn.silu(x)

def _sigmoid(x):
    return jax.nn.sigmoid(x)

def _layernorm(x, axis=-1, eps=1e-05):
    m = jnp.mean(x, axis=axis, keepdims=True)
    v = jnp.var(x, axis=axis, keepdims=True)
    return (x - m) / jnp.sqrt(v + eps)

def _scatter_add(tgt, idx, src, axis=0):
    return tgt.at[idx].add(src)

def _segment_sum(src, seg, n):
    return jax.ops.segment_sum(src, seg, n)
kernel_name = 'mk_macaron_d1_jaxref_r8_720997'

def setup_inputs(seed: int=0):
    np.random.seed(seed)
    _w = jnp.asarray

    def _L0_attn_setup():
        import jax, jax.numpy as jnp
        import numpy as np
        B, L, C, H, WS = (8, 128, 128, 16, 128)
        HD = C // H

        def _local_mask(seq_len, window_size):
            idx = jnp.arange(seq_len)
            return jnp.abs(idx[:, None] - idx[None, :]) > window_size // 2
        key = jax.random.key(seed)
        k0, k1, k2 = jax.random.split(key, 3)
        x = jax.random.normal(k0, (B, L, C), jnp.float32)
        in_proj_w = jax.random.normal(k1, (3 * C, C), jnp.float32) * 0.02
        in_proj_b = jnp.zeros((3 * C,), jnp.float32)
        out_w = jax.random.normal(k2, (C, C), jnp.float32) * 0.02
        out_b = jnp.zeros((C,), jnp.float32)
        return {'x': x, 'in_proj_w': in_proj_w, 'in_proj_b': in_proj_b, 'out_w': out_w, 'out_b': out_b}
    _L0_attn_in = _L0_attn_setup()

    def _L0_ffn_setup():
        import jax, jax.numpy as jnp
        import numpy as np
        TOP_K = 2
        key = jax.random.key(seed)
        k_x, k_g, k_w1, k_w2, k_w3 = jax.random.split(key, 5)
        B, S, D, H, E = (2, 64, 128, 64, 8)
        x = jax.random.normal(k_x, (B, S, D), dtype=jnp.float32)
        gate_w = jax.random.normal(k_g, (D, E), dtype=jnp.float32) * D ** (-0.5)
        w1 = jax.random.normal(k_w1, (E, D, H), dtype=jnp.float32) * 0.02
        w2 = jax.random.normal(k_w2, (E, H, D), dtype=jnp.float32) * 0.02
        w3 = jax.random.normal(k_w3, (E, D, H), dtype=jnp.float32) * 0.02
        return {'x': x, 'gate_w': gate_w, 'w1': w1, 'w2': w2, 'w3': w3}
    _L0_ffn_in = _L0_ffn_setup()
    _d = {'L0_attn_x': _L0_attn_in['x'], 'L0_attn_in_proj_w': _L0_attn_in['in_proj_w'], 'L0_attn_in_proj_b': _L0_attn_in['in_proj_b'], 'L0_attn_out_w': _L0_attn_in['out_w'], 'L0_attn_out_b': _L0_attn_in['out_b'], 'L0_ffn_gate_w': _L0_ffn_in['gate_w'], 'L0_ffn_w1': _L0_ffn_in['w1'], 'L0_ffn_w2': _L0_ffn_in['w2'], 'L0_ffn_w3': _L0_ffn_in['w3']}
    _x0 = _d['L0_attn_x']
    _d['L0_attn_x'] = jax.random.normal(jax.random.fold_in(jax.random.key(seed), 1), (1, 2048, 128), dtype=_x0.dtype)
    del _x0
    return _d

def reference(L0_attn_x, L0_attn_in_proj_w, L0_attn_in_proj_b, L0_attn_out_w, L0_attn_out_b, L0_ffn_gate_w, L0_ffn_w1, L0_ffn_w2, L0_ffn_w3):

    def _L0_attn_ref(x, in_proj_w, in_proj_b, out_w, out_b):
        import jax, jax.numpy as jnp
        import numpy as np
        B, L, C, H, WS = (8, 128, 128, 16, 128)
        HD = C // H

        def _local_mask(seq_len, window_size):
            idx = jnp.arange(seq_len)
            return jnp.abs(idx[:, None] - idx[None, :]) > window_size // 2
        Bc, Lc, Cc = x.shape
        qkv = x @ in_proj_w.T + in_proj_b
        q, k, v = jnp.split(qkv, 3, axis=-1)
        to_heads = lambda t: t.reshape(Bc, Lc, H, HD).transpose(0, 2, 1, 3)
        q, k, v = (to_heads(q), to_heads(k), to_heads(v))
        scale = 1.0 / np.sqrt(HD).astype(np.float32)
        scores = jnp.einsum('bhqd,bhkd->bhqk', q, k) * scale
        blocked = _local_mask(Lc, WS)
        scores = jnp.where(blocked[None, None], -jnp.inf, scores)
        attn = jax.nn.softmax(scores, axis=-1)
        out = jnp.einsum('bhqk,bhkd->bhqd', attn, v)
        out = out.transpose(0, 2, 1, 3).reshape(Bc, Lc, Cc)
        return out @ out_w.T + out_b

    def _L0_ffn_ref(x, gate_w, w1, w2, w3):
        import jax, jax.numpy as jnp
        import numpy as np
        TOP_K = 2
        B, S, D = x.shape
        E = gate_w.shape[1]
        xf = x.reshape(B * S, D)
        T = B * S
        logits = xf @ gate_w
        scores = jax.nn.softmax(logits, axis=-1)
        top_scores, top_idx = jax.lax.top_k(scores, TOP_K)
        scale = jnp.zeros((T, E), dtype=x.dtype).at[jnp.arange(T)[:, None], top_idx].set(top_scores)
        xs = scale.T[:, :, None] * xf[None, :, :]
        h = jax.nn.silu(jnp.einsum('etd,edh->eth', xs, w1)) * jnp.einsum('etd,edh->eth', xs, w3)
        y = jnp.einsum('eth,ehd->etd', h, w2)
        out = y.sum(axis=0)
        return out.reshape(B, S, D)
    x = L0_attn_x
    x = x + 0.5 * _L0_ffn_ref(_layernorm(x, axis=-1), L0_ffn_gate_w, L0_ffn_w1, L0_ffn_w2, L0_ffn_w3)
    x = x + _L0_attn_ref(_layernorm(x, axis=-1), L0_attn_in_proj_w, L0_attn_in_proj_b, L0_attn_out_w, L0_attn_out_b)
    x = x + 0.5 * _L0_ffn_ref(_layernorm(x, axis=-1), L0_ffn_gate_w, L0_ffn_w1, L0_ffn_w2, L0_ffn_w3)
    return x

_drawn_inputs = setup_inputs


def setup_inputs(seed=0):
    import zlib

    import numpy as np

    out = dict(_drawn_inputs(seed))
    spreads = {'L0_attn_in_proj_b': (0.0, 0.349), 'L0_attn_out_b': (0.0, 0.1)}
    factors = {'L0_attn_in_proj_w': 8.0,
     'L0_ffn_gate_w': 8.0,
     'L0_ffn_w1': 8.0,
     'L0_ffn_w2': 8.0,
     'L0_ffn_w3': 8.0}
    for name, (base, spread) in spreads.items():
        noise = np.random.default_rng([zlib.crc32(name.encode()), seed]).standard_normal(out[name].shape)
        drawn = base * np.exp(spread * noise) if base else spread * noise
        out[name] = jnp.asarray(drawn.astype(out[name].dtype))
    for name, factor in factors.items():
        out[name] = (out[name] * factor).astype(out[name].dtype)
    return out
```

```python
from contextlib import ExitStack

import numpy as np

import concourse.bass as bass
from concourse import mybir

F32 = mybir.dt.float32
BF16 = mybir.dt.bfloat16
U32 = mybir.dt.uint32
ALU = mybir.AluOpType
ACT = mybir.ActivationFunctionType
AX = mybir.AxisListType.X

T, C = 2048, 128
P = 128
NT = T // P
H, HD = 16, 8
E, FH = 8, 64
EH = E * FH
NCH = EH // P
HALF = 64
TP = T + 2 * HALF
W = 2 * P
VD = HD + 1
PAIRS = H // 2
GROUPS = ((0, 3), (1, 2), (2, 1))
NPROD = 6
NSAVE = 2 * len(GROUPS) + 1
R_DATA = NPROD * HD
R_VALID = R_DATA + 1
R_ALL = R_VALID + 3
FLOOR = -3.0e38
BIG = -1.0e38
EPS = 1e-5
LAG = 16
NBUF = 4


class Shared:
    pass


class Tile:

    def __init__(self, i, at, ring):
        self.i, self.at, self.ring = i, at, ring

    def __add__(self, n):
        return Tile(self.i, self.at + n, self.ring)

    def __sub__(self, n):
        return Tile(self.i, self.at - n, self.ring)

    @property
    def n(self):
        return self.i * self.ring + self.at

    @property
    def slot(self):
        return self.at % self.ring

    @property
    def round(self):
        return self.i + self.at // self.ring

    @property
    def exists(self):
        return not isinstance(self.i, int) or 0 <= self.at < NT


def count(value):
    return max(value, 0) if isinstance(value, int) else value


def register(engine, value):
    return value if isinstance(value, int) else engine.to_reg(value)


def run_tiles(engine, first, last, lo, rounds, ring, body):
    for at in range(first, lo):
        body(Tile(0, at, ring))
    with engine.Fori(0, rounds) as i:
        for k in range(ring):
            body(Tile(i, lo + k, ring))
    for at in range(lo + ring * rounds, last):
        body(Tile(0, at, ring))


def allocate(nc, ctx):
    m = Shared()

    def sb(name, shape, dt=F32):
        return ctx.enter_context(nc.sbuf_tensor(name, shape, dt))

    m.x = [sb(f"x{i}", [P, NT, C]) for i in range(4)]
    m.x1b = sb("x1b", [P, NT, C])
    m.gate = sb("gate", [C, E])
    m.w1 = sb("w1", [C, EH])
    m.w3 = sb("w3", [C, EH])
    m.w2 = sb("w2", [P, NCH, C])
    m.wqkv = sb("wqkv", [C, 3 * C])
    m.wo = sb("wo", [C, C])
    m.bqk = sb("bqk", [C, 2])
    m.bqs = sb("bqs", [C, 1])
    m.bv = sb("bv", [P, C])
    m.bo = sb("bo", [P, C])
    m.ident = sb("ident", [P, P])
    m.identb = sb("identb", [P, P], BF16)
    m.band = sb("band", [P, W], BF16)
    m.bandT = sb("bandT", [P, W], BF16)
    m.iota = sb("iota", [P, E])
    m.mhalf = sb("mhalf", [P, 1])
    m.zerof = sb("zerof", [P, 1])
    m.zero = sb("zero", [P, 6 * HALF], BF16)
    m.qs = [sb(f"qs{i}", [P, H, P], BF16) for i in range(NBUF)]
    m.ks = [sb(f"ks{i}", [P, H, W], BF16) for i in range(NBUF)]
    m.loaded = ctx.enter_context(nc.semaphore("s_loaded"))
    m.psum = ctx.enter_context(nc.psum_tensor("psum", [P, 8, 512], F32))
    return m


def load(nc, m, d):
    with ExitStack() as ctx:
        s_set = ctx.enter_context(nc.semaphore("s_set"))
        s_zero = ctx.enter_context(nc.semaphore("s_zero"))
        s_pad = ctx.enter_context(nc.semaphore("s_pad"))
        block = ctx.enter_context(nc.Block())

        @block.sync
        def _(sp):
            xv = d.x.rearrange("(t p) c -> p t c", p=P)
            n = 0
            for q in range(4):
                sp.dma_start(m.x[0][:, 4 * q:4 * q + 4, :], xv[:, 4 * q:4 * q + 4, :]).then_inc(m.loaded, 16)
                n += 16
            for dst, src in ((m.ident[:], d.ident), (m.gate[:], d.gate), (m.w1[:], d.w1), (m.w3[:], d.w3),
                             (m.w2[:], d.w2.rearrange("(n p) c -> p n c", p=P)), (m.wqkv[:, 0:2 * C], d.wqk), (m.wqkv[:, 2 * C:3 * C], d.wv),
                             (m.wo[:], d.wo), (m.identb[:], d.identb), (m.band[:], d.band), (m.bandT[:], d.bandT), (m.iota[:], d.iota),
                             (m.bqk[:], d.bqk),
                             (m.bv[:], d.bv.partition_broadcast(P)),
                             (m.bo[:], d.bo.partition_broadcast(P))):
                sp.dma_start(dst, src).then_inc(m.loaded, 16)
                n += 16
            sp.wait_ge(s_set, 1)
            for at in (0, T + HALF):
                sp.dma_start(d.scrk[0:R_DATA, :, at:at + HALF].rearrange("r h t -> (r h) t")
                             .rearrange("(p k) t -> p k t", k=6),
                             m.zero[:, :].rearrange("p (k t) -> p k t", k=6)).then_inc(s_pad, 16)
                sp.dma_start(d.scrv[at:at + HALF, :],
                             m.zero[0:HALF, 0:2 * H * VD].bitcast(F32)).then_inc(s_pad, 16)
            sp.wait_ge(s_zero, 2 * NBUF)
            for i in range(NBUF):
                sp.dma_start(m.qs[i][R_DATA:R_VALID, :, :], d.ones[0:1, 0:H * P].rearrange("a (h q) -> a h q", h=H)
                             ).then_inc(m.loaded, 16)
                sp.dma_start(m.ks[i][R_VALID:R_ALL, :, :], d.ones.rearrange("a (h q) -> a h q", h=H)
                             ).then_inc(m.loaded, 16)
                n += 32
            sp.dma_start(d.scrk[R_DATA:R_VALID, :, :], d.valid).then_inc(m.loaded, 16)
            n += 16
            m.n_loaded = n
            sp.wait_ge(m.loaded, n)
            sp.wait_ge(s_pad, 64)

        @block.gpsimd
        def _(pool):
            for i in range(NBUF):
                nc.gpsimd.memset(m.qs[i][:].bitcast(F32), 0.0).then_inc(s_zero, 1)
                if i:
                    nc.gpsimd.memset(m.ks[i][:].bitcast(F32), 0.0).then_inc(s_zero, 1)

        @block.vector
        def _(dve):
            nc.vector.memset(m.zero[:], 0.0).then_inc(s_set, 1)
            nc.vector.memset(m.mhalf[:], -0.5).then_inc(s_set, 1)
            nc.vector.memset(m.zerof[:], 0.0).then_inc(s_set, 1)
            nc.vector.memset(m.ks[0][:].bitcast(F32), 0.0).then_inc(s_zero, 1)
            nc.vector.memset(m.psum[:, :, :].rearrange("p a b -> p (a b)"), 0.0).then_inc(s_set, 1)


def ffn(nc, m, d, which):
    first = which == 0
    X, Y = (m.x[0], m.x[1]) if first else (m.x[2], m.x[3])
    R = 4
    with ExitStack() as ctx:
        def sb(name, shape, dt=F32):
            return ctx.enter_context(nc.sbuf_tensor(f"{name}_{which}", shape, dt))

        def sem(name):
            return ctx.enter_context(nc.semaphore(f"{name}_{which}"))

        bnst = sb("bnst", [P, R, 6])
        mv = sb("mv", [P, R, 2])
        ve = sb("ve", [P, R, 1])
        nmean = sb("nmean", [P, R, 1])
        rstd = sb("rstd", [P, R, 1])
        shift = sb("shift", [P, R, 1])
        xn = sb("xn", [P, R, C])
        xnT = sb("xnT", [C, R, P])
        top = sb("top", [P, R, 8])
        topi = sb("topi", [P, R, 8], U32)
        nmax = sb("nmax", [P, R, 1])
        idx = sb("idx", [P, R, 2])
        hot1 = sb("hot1", [P, R, E])
        hot = sb("hot", [P, R, E])
        ex = sb("ex", [P, R, E])
        esum = sb("esum", [P, R, 1])
        rsum = sb("rsum", [P, R, 1])
        sc = sb("sc", [P, R, E])
        u = sb("u", [P, R, EH])
        v = sb("v", [P, R, EH])
        uv = sb("uv", [P, R, EH])
        th = sb("th", [P, R, EH])
        h = sb("h", [P, R, EH])
        hT = sb("hT", [P, R, NCH, P])
        if first:
            bnst2 = sb("bnst2", [P, R, 6])
            mv2 = sb("mv2", [P, R, 2])
            ve2 = sb("ve2", [P, R, 1])
            nmean2 = sb("nmean2", [P, R, 1])
            rstd2 = sb("rstd2", [P, R, 1])
            shift2 = sb("shift2", [P, R, 1])
            xn2 = sb("xn2", [P, R, C])
            xn2T = sb("xn2T", [C, R, P])
            qk = sb("qk", [C, R, 2, P])
            rest = sb("rest", [C, R, 2, P])
            parts = sb("parts", [C, R, 3, 2, P], BF16)
            vaug = sb("vaug", [P, R, H, VD])

        A, B, XT, LG, HT, YP0, YP1, QKV = (m.psum[:, i, :] for i in range(8))
        YP = (YP0, YP1)

        s = Shared()
        s.bnst = sem("s_bnst")
        s.stats = sem("s_stats")
        s.ve = sem("s_ve")
        s.nmean = sem("s_nmean")
        s.rstd = sem("s_rstd")
        s.shift = sem("s_shift")
        s.xn = sem("s_xn")
        s.xnT_ps = sem("s_xnT_ps")
        s.xnT = sem("s_xnT")
        s.logits = sem("s_logits")
        s.top = sem("s_top")
        s.topi = sem("s_topi")
        s.nmax = sem("s_nmax")
        s.idx = sem("s_idx")
        s.hot1 = sem("s_hot1")
        s.hot = sem("s_hot")
        s.ex = sem("s_ex")
        s.rsum = sem("s_rsum")
        s.sc = sem("s_sc")
        s.a = sem("s_a")
        s.b = sem("s_b")
        s.u = sem("s_u")
        s.v = sem("s_v")
        s.uv = sem("s_uv")
        s.th = sem("s_th")
        s.h = sem("s_h")
        s.hT_ps = sem("s_hT_ps")
        s.hT = sem("s_hT")
        s.y_ps = sem("s_y_ps")
        s.y = sem("s_y")
        s.bnst2 = sem("s_bnst2")
        s.stats2 = sem("s_stats2")
        s.ve2 = sem("s_ve2")
        s.nmean2 = sem("s_nmean2")
        s.rstd2 = sem("s_rstd2")
        s.shift2 = sem("s_shift2")
        s.xn2 = sem("s_xn2")
        s.xn2T_ps = sem("s_xn2T_ps")
        s.xn2T = sem("s_xn2T")
        s.qkv_ps = sem("s_qkv_ps")
        s.qk = sem("s_qk")
        s.part0 = sem("s_part0")
        s.rest = sem("s_rest")
        s.part1 = sem("s_part1")
        s.part2 = sem("s_part2")
        s.vaug = sem("s_vaug")
        s.set = sem("s_set")
        s.free, s.out = ([sem(f"s_{name}{i}") for i in range(R)] for name in ("free", "out"))
        block = ctx.enter_context(nc.Block())
        if first:
            RANGE = (-3, NT + 6, 5, 2, R)
        else:
            RANGE = (-3, NT + 3, 5, 2, R)

        @block.vector
        def _(dve):
            if first:
                nc.vector.tensor_scalar(m.bqs[:], m.bqk[:, 0:1], HD ** -0.5, None, ALU.mult).then_inc(s.set, 1)
                for i in range(R):
                    nc.vector.memset(vaug[:, i], 1.0).then_inc(s.free[i], 16)

            def body(t):
                n, k, k1, k3 = t.n, t.slot, (t + 1).slot, (t + 3).slot
                b1, b3, b5 = (t - 1).slot, (t - 3).slot, (t - 5).slot
                lg = LG[:, 0:E]
                scale = sc[:, k, :].unsqueeze(2).broadcast_to([P, E, FH])
                if (t + 3).exists:
                    nc.vector.bn_stats(bnst[:, k3, :], X[:, (t + 3).n, :]).then_inc(s.bnst, 1)
                if (t + 1).exists:
                    value = register(dve, n + 2)
                    dve.wait_ge(m.loaded, m.n_loaded)
                    dve.wait_ge(s.logits, value)
                    nc.vector.max(top[:, k1, :], lg).then_inc(s.top, 1)
                if (t + 3).exists:
                    value = register(dve, n + 4)
                    dve.wait_ge(m.loaded, m.n_loaded)
                    dve.wait_ge(s.bnst, value)
                    nc.vector.bn_aggr(mv[:, k3, :], bnst[:, k3, :]).then_inc(s.stats, 1)
                if (t + 1).exists:
                    dve.wait_ge(s.top, n + 2)
                    nc.vector.tensor_scalar(nmax[:, k1, :], top[:, k1, 0:1], -1.0, None, ALU.mult).then_inc(s.nmax, 1)
                    nc.vector.max_index(topi[:, k1, :], top[:, k1, :], lg).then_inc(s.topi, 1)
                if (t - 3).exists:
                    dve.wait_ge(s.y_ps, n - 2)
                    nc.vector.scalar_tensor_tensor(Y[:, (t - 3).n, :], YP[(t - 3).at % 2][:, 0:C], 0.25,
                                                   X[:, (t - 3).n, :], ALU.mult, ALU.add).then_inc(s.y, 1)
                if (t + 3).exists:
                    dve.wait_ge(s.stats, n + 4)
                    nc.vector.tensor_scalar(ve[:, k3, :], mv[:, k3, 1:2], EPS, None, ALU.add).then_inc(s.ve, 1)
                    nc.vector.tensor_scalar(nmean[:, k3, :], mv[:, k3, 0:1], -1.0, None, ALU.mult
                                            ).then_inc(s.nmean, 1)
                if (t + 1).exists:
                    dve.wait_ge(s.topi, n + 2)
                    nc.vector.tensor_copy(idx[:, k1, :], topi[:, k1, 0:2]).then_inc(s.idx, 1)
                if first and (t - 3).exists:
                    value = register(dve, n - 2)
                    dve.wait_ge(m.loaded, m.n_loaded)
                    dve.wait_ge(s.y, value)
                    nc.vector.bn_stats(bnst2[:, b3, :], Y[:, (t - 3).n, :]).then_inc(s.bnst2, 1)
                if (t + 1).exists:
                    dve.wait_ge(s.idx, n + 2)
                    nc.vector.tensor_scalar(hot1[:, k1, :], m.iota[:], idx[:, k1, 0:1], None,
                                            ALU.is_equal).then_inc(s.hot1, 1)
                if first and (t - 3).exists:
                    value = register(dve, n - 2)
                    dve.wait_ge(m.loaded, m.n_loaded)
                    dve.wait_ge(s.bnst2, value)
                    nc.vector.bn_aggr(mv2[:, b3, :], bnst2[:, b3, :]).then_inc(s.stats2, 1)
                if (t - 1).exists:
                    dve.wait_ge(s.th, n)
                    dve.wait_ge(s.uv, n)
                    nc.vector.scalar_tensor_tensor(h[:, b1, :], th[:, b1, :], 1.0, uv[:, b1, :],
                                                   ALU.add, ALU.mult).then_inc(s.h, 1)
                if first and (t - 3).exists:
                    dve.wait_ge(s.stats2, n - 2)
                    nc.vector.tensor_scalar(ve2[:, b3, :], mv2[:, b3, 1:2], EPS, None, ALU.add).then_inc(s.ve2, 1)
                    nc.vector.tensor_scalar(nmean2[:, b3, :], mv2[:, b3, 0:1], -1.0, None, ALU.mult
                                            ).then_inc(s.nmean2, 1)
                if t.exists:
                    dve.wait_ge(s.a, n + 1)
                    dve.wait_ge(s.sc, n + 1)
                    nc.vector.tensor_tensor(u[:, k, :].rearrange("p (e f) -> p e f", e=E),
                                            A.rearrange("p (e f) -> p e f", e=E), scale, ALU.mult).then_inc(s.u, 1)
                if (t + 1).exists:
                    dve.wait_ge(s.hot1, n + 2)
                    nc.vector.scalar_tensor_tensor(hot[:, k1, :], m.iota[:], idx[:, k1, 1:2], hot1[:, k1, :],
                                                   ALU.is_equal, ALU.add).then_inc(s.hot, 1)
                    dve.wait_ge(s.ex, n + 2)
                    nc.vector.reciprocal(rsum[:, k1, :], esum[:, k1, :]).then_inc(s.rsum, 1)
                if first and (t - 5).exists:
                    dve.wait_ge(s.qkv_ps, n - 4)
                    dve.wait_ge(s.qk, n - 4)
                    dve.wait_ge(s.free[b5], 16 * NSAVE * (t - 5).round + 16)
                    nc.vector.tensor_tensor(vaug[:, b5, :, 0:HD],
                                            QKV[:, 2 * P:3 * P].rearrange("p (h d) -> p h d", h=H),
                                            m.bv[:].rearrange("p (h d) -> p h d", h=H), ALU.add).then_inc(s.vaug, 1)
                if t.exists:
                    dve.wait_ge(s.b, n + 1)
                    nc.vector.tensor_tensor(v[:, k, :].rearrange("p (e f) -> p e f", e=E),
                                            B.rearrange("p (e f) -> p e f", e=E), scale, ALU.mult).then_inc(s.v, 1)
                if (t + 1).exists:
                    dve.wait_ge(s.rsum, n + 2)
                    dve.wait_ge(s.hot, n + 2)
                    nc.vector.scalar_tensor_tensor(sc[:, k1, :], ex[:, k1, :], rsum[:, k1, :], hot[:, k1, :],
                                                   ALU.mult, ALU.mult).then_inc(s.sc, 1)

            run_tiles(dve, *RANGE, body)

        @block.gpsimd
        def _(pool):
            def body(t):
                n, k, k3 = t.n, t.slot, (t + 3).slot
                b3, b5 = (t - 3).slot, (t - 5).slot
                if (t + 3).exists:
                    pool.wait_ge(s.ve, n + 4)
                    nc.gpsimd.tensor_tensor(rstd[:, k3, :], ve[:, k3, :], m.mhalf[:], ALU.pow).then_inc(s.rstd, 1)
                    pool.wait_ge(s.rstd, n + 4)
                    pool.wait_ge(s.nmean, n + 4)
                    nc.gpsimd.tensor_tensor(shift[:, k3, :], nmean[:, k3, :], rstd[:, k3, :], ALU.mult
                                            ).then_inc(s.shift, 1)
                if first and (t - 5).exists:
                    pool.wait_ge(s.part0, n - 4)
                    nc.gpsimd.tensor_tensor(rest[:, b5], qk[:, b5], parts[:, b5, 0], ALU.subtract
                                            ).then_inc(s.rest, 1)
                if first and (t - 3).exists:
                    pool.wait_ge(s.ve2, n - 2)
                    nc.gpsimd.tensor_tensor(rstd2[:, b3, :], ve2[:, b3, :], m.mhalf[:], ALU.pow).then_inc(s.rstd2, 1)
                    pool.wait_ge(s.rstd2, n - 2)
                    pool.wait_ge(s.nmean2, n - 2)
                    nc.gpsimd.tensor_tensor(shift2[:, b3, :], nmean2[:, b3, :], rstd2[:, b3, :], ALU.mult
                                            ).then_inc(s.shift2, 1)
                if t.exists:
                    pool.wait_ge(s.v, n + 1)
                    nc.gpsimd.tensor_tensor(uv[:, k, :], u[:, k, :], v[:, k, :], ALU.mult).then_inc(s.uv, 1)
                if first and (t - 5).exists:
                    pool.wait_ge(s.part1, n - 4)
                    nc.gpsimd.tensor_tensor(parts[:, b5, 2], rest[:, b5], parts[:, b5, 1],
                                            ALU.subtract).then_inc(s.part2, 1)

            run_tiles(pool, *RANGE, body)

        @block.scalar
        def _(act):
            if first:
                act.wait_ge(s.set, 1)

            def body(t):
                n, k = t.n, t.slot
                if first and (t - 5).exists:
                    b5 = (t - 5).slot
                    act.wait_ge(s.qkv_ps, n - 4)
                    nc.scalar.activation(qk[:, b5, 0, :], QKV[:, 0:P], ACT.Identity, bias=m.bqs[:], scale=HD ** -0.5)
                    nc.scalar.activation(qk[:, b5, 1, :], QKV[:, P:2 * P], ACT.Identity,
                                         bias=m.bqk[:, 1:2]).then_inc(s.qk, 1)
                if (t - 2).exists:
                    b2 = (t - 2).slot
                    act.wait_ge(s.hT_ps, n - 1)
                    nc.scalar.activation(hT[:, b2].rearrange("p n q -> p (n q)"), HT, ACT.Copy).then_inc(s.hT, 1)
                if first and (t - 4).exists:
                    b4 = (t - 4).slot
                    act.wait_ge(s.xn2T_ps, n - 3)
                    nc.scalar.activation(xn2T[:, b4, :], XT[:, P:2 * P], ACT.Copy).then_inc(s.xn2T, 1)
                if (t + 1).exists:
                    k1 = (t + 1).slot
                    act.wait_ge(s.nmax, n + 2)
                    act.wait_ge(s.topi, n + 2)
                    nc.scalar.activation(ex[:, k1, :], LG[:, 0:E], ACT.Exp, bias=nmax[:, k1, :],
                                         accum_out=esum[:, k1, :]).then_inc(s.ex, 1)
                if first and (t - 5).exists:
                    act.wait_ge(s.qk, n - 4)
                    act.wait_ge(s.free[b5], 16 * NSAVE * (t - 5).round + 16)
                    nc.scalar.activation(parts[:, b5, 0], qk[:, b5], ACT.Copy).then_inc(s.part0, 1)
                if (t + 2).exists:
                    k2 = (t + 2).slot
                    act.wait_ge(s.xnT_ps, n + 3)
                    nc.scalar.activation(xnT[:, k2, :], XT[:, 0:P], ACT.Copy).then_inc(s.xnT, 1)
                if t.exists:
                    act.wait_ge(s.u, n + 1)
                    nc.scalar.activation(th[:, k, :], u[:, k, :], ACT.Tanh, scale=0.5).then_inc(s.th, 1)
                if (t + 3).exists:
                    k3 = (t + 3).slot
                    act.wait_ge(s.shift, n + 4)
                    nc.scalar.activation(xn[:, k3, :], X[:, (t + 3).n, :], ACT.Identity, bias=shift[:, k3, :],
                                         scale=rstd[:, k3, :]).then_inc(s.xn, 1)
                if first and (t - 5).exists:
                    act.wait_ge(s.rest, n - 4)
                    nc.scalar.activation(parts[:, b5, 1], rest[:, b5], ACT.Copy).then_inc(s.part1, 1)
                if first and (t - 3).exists:
                    b3 = (t - 3).slot
                    act.wait_ge(s.shift2, n - 2)
                    nc.scalar.activation(xn2[:, b3, :], Y[:, (t - 3).n, :], ACT.Identity, bias=shift2[:, b3, :],
                                         scale=rstd2[:, b3, :]).then_inc(s.xn2, 1)

            run_tiles(act, *RANGE, body)

        @block.tensor
        def _(pe):
            def body(t):
                n, k = t.n, t.slot
                if (t - 2).exists:
                    b2 = (t - 2).slot
                    pe.wait_ge(s.h, n - 1)
                    for c in range(NCH):
                        last = nc.tensor.transpose(HT[:, c * P:(c + 1) * P], h[:, b2, c * P:(c + 1) * P], m.ident[:])
                    last.then_inc(s.hT_ps, 1)
                if first and (t - 4).exists:
                    b4 = (t - 4).slot
                    pe.wait_ge(s.xn2, n - 3)
                    pe.wait_ge(s.xnT, min(n + 2, NT) if isinstance(n, int) else n + 2)
                    nc.tensor.transpose(XT[:, P:2 * P], xn2[:, b4, :], m.ident[:]).then_inc(s.xn2T_ps, 1)
                if t.exists:
                    pe.wait_ge(s.xnT, n + 1)
                    pe.wait_ge(s.u, count(n))
                    nc.tensor.matmul(A, xnT[:, k, :], m.w1[:], start=True, stop=True).then_inc(s.a, 1)
                if (t + 2).exists:
                    pe.wait_ge(s.xn, n + 3)
                    pe.wait_ge(s.xnT, count(n + 2))
                    if first:
                        pe.wait_ge(s.xn2T, count(n - 3))
                    nc.tensor.transpose(XT[:, 0:P], xn[:, (t + 2).slot, :], m.ident[:]).then_inc(s.xnT_ps, 1)
                if t.exists:
                    pe.wait_ge(s.v, count(n))
                    nc.tensor.matmul(B, xnT[:, k, :], m.w3[:], start=True, stop=True).then_inc(s.b, 1)
                if (t - 2).exists:
                    pe.wait_ge(s.hT, n - 1)
                    pe.wait_ge(s.y, count(n - 3))
                    for c in range(NCH):
                        last = nc.tensor.matmul(YP[t.at % 2][:, 0:C], hT[:, b2, c, :], m.w2[:, c, :],
                                                start=(c == 0), stop=(c == NCH - 1))
                    last.then_inc(s.y_ps, 1)
                if first and (t - 4).exists:
                    pe.wait_ge(s.xn2T, n - 3)
                    pe.wait_ge(s.vaug, count(n - 4))
                    for c in range(2):
                        nc.tensor.matmul(QKV[:, c * P:(c + 1) * P], m.wqkv[:, c * C:(c + 1) * C], xn2T[:, b4, :],
                                         start=True, stop=True)
                    nc.tensor.matmul(QKV[:, 2 * P:3 * P], xn2T[:, b4, :], m.wqkv[:, 2 * C:3 * C],
                                     start=True, stop=True).then_inc(s.qkv_ps, 1)
                if (t + 2).exists:
                    pe.wait_ge(s.xnT, n + 3)
                    pe.wait_ge(s.ex, count(n + 2))
                    nc.tensor.matmul(LG[:, 0:E], xnT[:, (t + 2).slot, :], m.gate[:],
                                     start=True, stop=True).then_inc(s.logits, 1)

            run_tiles(pe, *RANGE, body)

        @block.sync
        def _(sp):
            if first:
                def body(t):
                    at = HALF + t.n * P
                    sp.wait_ge(s.part2, t.n + 1)
                    row = 0
                    for kpart, nq in GROUPS:
                        rows = slice(row * HD, (row + nq) * HD)
                        row += nq
                        sp.dma_start(d.scrk[rows, :, bass.ds(at, P)].rearrange("(p d) h t -> (d h) p t", p=nq),
                                     parts[:, t.slot, kpart, 1, :].unsqueeze(1).broadcast_to([C, nq, P])
                                     ).then_inc(s.free[t.slot], 16)
                        sp.dma_start(d.scrq[rows, :, bass.ds(t.n * P, P)].rearrange("(p d) h t -> (d h) p t", p=nq),
                                     parts[:, t.slot, 0:nq, 0, :]).then_inc(s.free[t.slot], 16)
                    sp.wait_ge(s.vaug, t.n + 1)
                    sp.dma_start(d.scrv[bass.ds(at, P), :],
                                 vaug[:, t.slot].rearrange("p h d -> p (h d)")).then_inc(s.free[t.slot], 16)

                run_tiles(sp, 0, NT, 0, NT // R, R, body)
                for i in range(R):
                    sp.wait_ge(s.free[i], 16 * NSAVE * NT // R + 16)
            else:
                def body(t):
                    sp.wait_ge(s.y, t.n + 1)
                    sp.dma_start(d.out[bass.ds(t.n * P, P), :], Y[:, t.n, :]).then_inc(s.out[t.slot], 16)

                run_tiles(sp, 0, NT, 0, NT // R, R, body)
                for i in range(R):
                    sp.wait_ge(s.out[i], 16 * NT // R)


def attention(nc, m, d):
    with ExitStack() as ctx:
        def sb(name, shape, dt=F32):
            return ctx.enter_context(nc.sbuf_tensor(name, shape, dt))

        def sem(name):
            return ctx.enter_context(nc.semaphore("s_" + name))

        qs, ks = m.qs, m.ks
        vs = [sb(f"vs{i}", [P, 2, H * VD]) for i in range(NBUF)]
        mx = [sb(f"mx{i}", [P, H]) for i in range(NBUF)]
        junk = sb("junk", [P, 4, W], BF16)
        nmr = [sb(f"nmr{i}", [H, P]) for i in range(NBUF)]
        nmp = [sb(f"nmp{i}", [H, 3, P], BF16) for i in range(NBUF)]
        pr = [sb(f"pr{i}", [P, 2, 2, P]) for i in range(4)]
        ot = sb("ot", [P, 4, P])
        rs = sb("rs", [P, H])
        o = sb("o", [P, C])
        oT = sb("oT", [C, P])

        SA = [m.psum[:, i, :] for i in range(2)]
        SB = [m.psum[:, 2 + i, :] for i in range(2)]
        OT, OX, NM, PJ = (m.psum[:, i, :] for i in range(4, 8))

        s = Shared()
        s.max = sem("t_max")
        s.mxT_ps = sem("t_mxT_ps")
        s.nmp0 = sem("t_nmp0")
        s.nmr = sem("t_nmr")
        s.nmp1 = sem("t_nmp1")
        s.nmp2 = sem("t_nmp2")
        s.x1b = sem("t_x1b")
        s.sa = sem("t_sa")
        s.sb = sem("t_sb")
        s.exp = sem("t_exp")
        s.pv = sem("t_pv")
        s.ot = sem("t_ot")
        s.ox = sem("t_ox")
        s.rs = sem("t_rs")
        s.o = sem("t_o")
        s.oT_ps = sem("t_oT_ps")
        s.oT = sem("t_oT")
        s.pj = sem("t_pj")
        s.x2 = sem("t_x2")
        s.q, s.k, s.v, s.nm_in = ([sem(f"t_{name}{i}") for i in range(NBUF)] for name in ("q", "k", "v", "nm_in"))
        block = ctx.enter_context(nc.Block())
        RANGE = (0, NT + 4, 4, 3, NBUF)

        def back(t, i, lag):
            return t - (lag - i + PAIRS - 1) // PAIRS, (i - lag) % PAIRS

        @block.sync
        def _(sp):
            def load(t):
                n, k = t.n, t.slot
                sp.wait_ge(s.sb, count(PAIRS * (n - NBUF + 1)))
                sp.dma_start(ks[k][0:R_VALID, :, :], d.scrk[:, :, bass.ds(n * P, W)]).then_inc(s.k[k], 16)
                sp.dma_start(qs[k][0:R_DATA, :, :], d.scrq[:, :, bass.ds(n * P, P)]).then_inc(s.q[k], 16)
                sp.wait_ge(s.pv, count(4 * (n - NBUF + 1)))
                sp.dma_start(vs[k][:], d.scrv[bass.ds(n * P, W), :].rearrange("(s p) c -> p s c", p=P)
                             ).then_inc(s.v[k], 16)

            def body(t):
                if (t + 1).exists:
                    load(t + 1)
                if (t - 1).exists:
                    k = (t - 1).slot
                    for p, part in enumerate((s.nmp0, s.nmp1, s.nmp2)):
                        sp.wait_ge(part, t.n)
                        sp.dma_start(qs[k][R_VALID + p:R_VALID + p + 1, :, :], nmp[k][:, p, :]
                                     ).then_inc(s.nm_in[k], 16)

            load(Tile(0, 0, NBUF))
            run_tiles(sp, 0, NT + 1, 3, 3, NBUF, body)

        @block.gpsimd
        def _(pool):
            def body(t):
                nc.gpsimd.tensor_tensor(m.x1b[:, t.n, :], m.x[1][:, t.n, :], m.bo[:], ALU.add).then_inc(s.x1b, 1)

            run_tiles(pool, 0, NT, 0, NT // NBUF, NBUF, body)

        @block.vector
        def _(dve):
            def body(t):
                n, k, j = t.n, t.slot, (t - 1).slot
                for i in range(PAIRS):
                    if t.exists:
                        value = register(dve, PAIRS * n + i + 1)
                        dve.wait_ge(m.loaded, m.n_loaded)
                        dve.wait_ge(s.sa, value)
                        for e in range(2):
                            nc.vector.tensor_tensor_reduce(
                                out=junk[:, (2 * i + e) % 4, :], in0=SA[i % 2][:, e * W:(e + 1) * W], in1=m.band[:],
                                scale=1.0, scalar=FLOOR, op0=ALU.add, op1=ALU.max,
                                accum_out=mx[k][:, 2 * i + e:2 * i + e + 1]).then_inc(s.max, 1)
                    if i == 1 and (t - 1).exists:
                        dve.wait_ge(s.mxT_ps, n)
                        dve.wait_ge(s.nm_in[(t - 4).slot], count(48 * (t - 4).round + 48))
                        nc.vector.tensor_scalar(nmp[j][:, 0, :], NM[0:H, 0:P], -1.0, None, ALU.mult
                                                ).then_inc(s.nmp0, 1)
                    if i == 2 and (t - 1).exists:
                        dve.wait_ge(s.nmp0, n)
                        nc.vector.scalar_tensor_tensor(nmr[j][:], NM[0:H, 0:P], -1.0, nmp[j][:, 0, :],
                                                       ALU.mult, ALU.subtract).then_inc(s.nmr, 1)
                    if i == 3 and (t - 1).exists:
                        dve.wait_ge(s.nmr, n)
                        nc.vector.tensor_copy(nmp[j][:, 1, :], nmr[j][:]).then_inc(s.nmp1, 1)
                    if i == 4 and (t - 1).exists:
                        dve.wait_ge(s.nmp1, n)
                        nc.vector.tensor_tensor(nmp[j][:, 2, :], nmr[j][:], nmp[j][:, 1, :], ALU.subtract
                                                ).then_inc(s.nmp2, 1)
                    if i == 4 and (t - 3).exists:
                        dve.wait_ge(s.ox, n - 2)
                        nc.vector.reciprocal(rs[:].rearrange("p (g j) -> p g j", g=4),
                                             OX.rearrange("p (g j c) -> p g j c", g=4, j=4)[:, :, :, HD]
                                             ).then_inc(s.rs, 1)
                    if i == 5 and (t - 3).exists:
                        dve.wait_ge(s.rs, n - 2)
                        nc.vector.tensor_tensor(o[:].rearrange("p (h d) -> p h d", h=H),
                                                OX.rearrange("p (h c) -> p h c", h=H)[:, :, 0:HD],
                                                rs[:].unsqueeze(2).broadcast_to([P, H, HD]), ALU.mult
                                                ).then_inc(s.o, 1)
                    if i == 0 and (t - 4).exists:
                        dve.wait_ge(s.pj, n - 3)
                        dve.wait_ge(s.x1b, n - 3)
                        nc.vector.tensor_tensor(m.x[2][:, (t - 4).n, :], PJ[:, P:P + C], m.x1b[:, (t - 4).n, :],
                                                ALU.add).then_inc(s.x2, 1)

            run_tiles(dve, *RANGE, body)

        @block.scalar
        def _(act):
            def body(t):
                for i in range(PAIRS):
                    if i == 2 and (t - 3).exists:
                        act.wait_ge(s.pv, 4 * (t - 2).n)
                        nc.scalar.activation(ot[:].rearrange("p g q -> p (g q)"), OT, ACT.Copy).then_inc(s.ot, 1)
                    if i == 7 and (t - 3).exists:
                        act.wait_ge(s.oT_ps, (t - 2).n)
                        nc.scalar.activation(oT[:], PJ[:, 0:P], ACT.Copy).then_inc(s.oT, 1)
                    tb, pb = back(t, i, LAG)
                    if tb.exists:
                        act.wait_ge(s.sb, PAIRS * tb.n + pb + 1)
                        act.wait_ge(s.pv, count(4 * tb.n + pb // 2 - 1))
                        nc.scalar.activation(pr[pb % 4][:].rearrange("p h s q -> p (h s q)"), SB[pb % 2],
                                             ACT.Exp).then_inc(s.exp, 1)

            run_tiles(act, *RANGE, body)

        @block.tensor
        def _(pe):
            def body(t):
                n, k = t.n, t.slot
                for i in range(PAIRS):
                    if t.exists:
                        if i == 0:
                            pe.wait_ge(s.q[k], 16 * (t.round + 1))
                            pe.wait_ge(s.k[k], 16 * (t.round + 1))
                        pe.wait_ge(s.max, count(2 * (PAIRS * n + i - 1)))
                        for e in range(2):
                            last = nc.tensor.matmul(SA[i % 2][:, e * W:(e + 1) * W], qs[k][0:R_VALID, 2 * i + e, :],
                                                    ks[k][0:R_VALID, 2 * i + e, :], start=True, stop=True)
                        last.then_inc(s.sa, 1)
                    if i == 1 and (t - 1).exists:
                        pe.wait_ge(s.max, 2 * PAIRS * n)
                        pe.wait_ge(s.nmr, count(n - 1))
                        nc.tensor.transpose(NM[0:H, 0:P], mx[(t - 1).slot][:], m.ident[:]).then_inc(s.mxT_ps, 1)
                    tb, pb = back(t, i, LAG)
                    if tb.exists:
                        kb = tb.slot
                        if pb == 0:
                            pe.wait_ge(s.nm_in[kb], 48 * (tb.round + 1))
                        pe.wait_ge(s.exp, count(PAIRS * tb.n + pb - 1))
                        bank = SB[pb % 2]
                        nc.tensor.matmul(bank.rearrange("p (h k) -> p h k", h=2), m.identb[:],
                                         m.bandT[:].unsqueeze(1).broadcast_to([P, 2, W]), start=True, stop=False)
                        for e in range(2):
                            for half in range(2):
                                at = (2 * e + half) * P
                                last = nc.tensor.matmul(bank[:, at:at + P],
                                                        ks[kb][:, 2 * pb + e, half * P:(half + 1) * P],
                                                        qs[kb][:, 2 * pb + e, :], start=False,
                                                        stop=(e == 1 and half == 1))
                        last.then_inc(s.sb, 1)
                    tv, pv = back(t, i, LAG + 2)
                    if pv % 2 == 1 and tv.exists:
                        kv, g = tv.slot, pv // 2
                        pe.wait_ge(s.exp, PAIRS * tv.n + pv + 1)
                        if g == 0:
                            pe.wait_ge(s.v[kv], 16 * (tv.round + 1))
                            pe.wait_ge(s.ot, count(tv.n))
                        for half in range(2):
                            for j in range(4):
                                hh = 4 * g + j
                                last = nc.tensor.matmul(OT[32 * j:32 * j + VD, g * P:(g + 1) * P],
                                                        vs[kv][:, half, hh * VD:(hh + 1) * VD],
                                                        pr[(2 * g + j // 2) % 4][:, j % 2, half, :],
                                                        start=(half == 0), stop=(half == 1))
                        last.then_inc(s.pv, 1)
                    if i == 3 and (t - 3).exists:
                        pe.wait_ge(s.ot, n - 2)
                        pe.wait_ge(s.o, n - 3)
                        for g in range(4):
                            last = nc.tensor.transpose(OX[:, g * P:(g + 1) * P], ot[:, g, :], m.ident[:])
                        last.then_inc(s.ox, 1)
                    if i == 6 and (t - 3).exists:
                        pe.wait_ge(s.o, n - 2)
                        pe.wait_ge(s.x2, n - 3)
                        nc.tensor.transpose(PJ[:, 0:P], o[:], m.ident[:]).then_inc(s.oT_ps, 1)
                    if i == 7 and (t - 3).exists:
                        pe.wait_ge(s.oT, n - 2)
                        nc.tensor.matmul(PJ[:, P:P + C], oT[:], m.wo[:], start=True, stop=True).then_inc(s.pj, 1)

            run_tiles(pe, *RANGE, body)


def build(nc, d):
    with ExitStack() as ctx:
        m = allocate(nc, ctx)
        load(nc, m, d)
        ffn(nc, m, d, 0)
        attention(nc, m, d)
        ffn(nc, m, d, 1)


def kernel(L0_attn_x, L0_attn_in_proj_w, L0_attn_in_proj_b, L0_attn_out_w, L0_attn_out_b, L0_ffn_gate_w, L0_ffn_w1,
           L0_ffn_w2, L0_ffn_w3):
    import concourse.bacc as _bacc
    import ml_dtypes
    from concourse.bass_utils import run_bass_kernel_spmd as _run

    def flat(a):
        return np.ascontiguousarray(a)

    i, c = np.arange(P)[:, None], np.arange(W)[None, :]
    band = np.where((c >= i) & (c <= i + 2 * HALF), 0.0, BIG).astype(ml_dtypes.bfloat16)
    q = c % P
    bandT = np.where(np.where(c < P, q <= i, q >= i), 0.0, BIG).astype(ml_dtypes.bfloat16)
    exists = np.full((1, H, TP), BIG)
    exists[:, :, HALF:HALF + T] = 0.0
    arrays = {
        "x": flat(L0_attn_x).reshape(T, C),
        "gate": flat(L0_ffn_gate_w),
        "w1": flat(np.transpose(L0_ffn_w1, (1, 0, 2))).reshape(C, EH),
        "w3": flat(np.transpose(L0_ffn_w3, (1, 0, 2))).reshape(C, EH),
        "w2": flat(L0_ffn_w2).reshape(EH, C),
        "wqk": flat(np.transpose(np.reshape(L0_attn_in_proj_w[0:2 * C], (2, H, HD, C)), (3, 0, 2, 1))).reshape(C, 2 * C),
        "wv": flat(np.transpose(L0_attn_in_proj_w[2 * C:])),
        "wo": flat(np.transpose(L0_attn_out_w)),
        "bqk": flat(np.transpose(np.reshape(L0_attn_in_proj_b[0:2 * C], (2, H, HD)), (2, 1, 0))).reshape(C, 2),
        "bv": flat(L0_attn_in_proj_b[2 * C:]),
        "bo": flat(L0_attn_out_b),
        "ident": np.eye(P, dtype=np.float32),
        "identb": np.eye(P).astype(ml_dtypes.bfloat16),
        "band": band,
        "bandT": bandT,
        "iota": flat(np.broadcast_to(np.arange(E, dtype=np.float32), (P, E))),
        "valid": exists.astype(ml_dtypes.bfloat16),
        "ones": np.ones((3, H * W), ml_dtypes.bfloat16),
    }
    nc = _bacc.Bacc("TRN2", target_bir_lowering=False, num_devices=1)

    def dram(name):
        a = arrays[name]
        return nc.dram_tensor(f"in_{name}", a.shape, mybir.dt.from_np(a.dtype), kind="ExternalInput").ap()

    d = Shared()
    d.x = dram("x")
    d.gate = dram("gate")
    d.w1 = dram("w1")
    d.w3 = dram("w3")
    d.w2 = dram("w2")
    d.wqk = dram("wqk")
    d.wv = dram("wv")
    d.wo = dram("wo")
    d.bqk = dram("bqk")
    d.bv = dram("bv")
    d.bo = dram("bo")
    d.ident = dram("ident")
    d.identb = dram("identb")
    d.band = dram("band")
    d.bandT = dram("bandT")
    d.iota = dram("iota")
    d.valid = dram("valid")
    d.ones = dram("ones")
    d.scrk = nc.dram_tensor("scrk", (R_VALID, H, TP), BF16, kind="Internal").ap()
    d.scrq = nc.dram_tensor("scrq", (R_DATA, H, T), BF16, kind="Internal").ap()
    d.scrv = nc.dram_tensor("scrv", (TP, H * VD), F32, kind="Internal").ap()
    d.out = nc.dram_tensor("out_0", (T, C), F32, kind="ExternalOutput").ap()
    build(nc, d)
    r = _run(nc, [{f"in_{name}": a for name, a in arrays.items()}], core_ids=[0])
    return r.results[0]["out_0"].reshape(1, T, C)
```

```python
from contextlib import ExitStack

import numpy as np

import concourse.bass as bass
from concourse import mybir

F32 = mybir.dt.float32
BF16 = mybir.dt.bfloat16
U32 = mybir.dt.uint32
ALU = mybir.AluOpType
ACT = mybir.ActivationFunctionType
AX = mybir.AxisListType.X

T, C = 2048, 128
P = 128
NT = T // P
H, HD = 16, 8
E, FH = 8, 64
EH = E * FH
NCH = EH // P
HALF = 64
TP = T + 2 * HALF
W = 2 * P
VD = HD + 1
PAIRS = H // 2
GROUPS = ((0, 3), (1, 2), (2, 1))
NPROD = 6
NSAVE = 2 * len(GROUPS) + 1
R = 4
R_DATA = NPROD * HD
R_VALID = R_DATA + 1
R_ALL = R_VALID + 3
FLOOR = -3.0e38
BIG = -1.0e38
EPS = 1e-5
LAG = 16
AHEAD = 3
NBUF = 4


class Shared:
    pass


class Tile:

    def __init__(self, i, at, ring):
        self.i, self.at, self.ring = i, at, ring

    def __add__(self, n):
        return Tile(self.i, self.at + n, self.ring)

    def __sub__(self, n):
        return Tile(self.i, self.at - n, self.ring)

    @property
    def n(self):
        return self.i * self.ring + self.at

    @property
    def slot(self):
        return self.at % self.ring

    @property
    def round(self):
        return self.i + self.at // self.ring

    @property
    def exists(self):
        return not isinstance(self.i, int) or 0 <= self.at < NT


def count(value):
    return max(value, 0) if isinstance(value, int) else value


def register(engine, value):
    return value if isinstance(value, int) else engine.to_reg(value)


def run_tiles(engine, first, last, lo, rounds, ring, body):
    for at in range(first, lo):
        body(Tile(0, at, ring))
    with engine.Fori(0, rounds) as i:
        for k in range(ring):
            body(Tile(i, lo + k, ring))
    for at in range(lo + ring * rounds, last):
        body(Tile(0, at, ring))


def allocate(nc, ctx):
    m = Shared()

    def sb(name, shape, dt=F32):
        return ctx.enter_context(nc.sbuf_tensor(name, shape, dt))

    m.x = [sb(f"x{i}", [P, NT, C]) for i in range(4)]
    m.x1b = sb("x1b", [P, NT, C])
    m.small = sb("small", [C, 2 * E + P])
    m.gate, m.iota, m.ident = m.small[:, 0:E], m.small[:, E:2 * E], m.small[:, 2 * E:2 * E + P]
    m.w13 = sb("w13", [C, 2 * EH])
    m.w1, m.w3 = m.w13[:, 0:EH], m.w13[:, EH:2 * EH]
    m.w = sb("w", [P, 2 * EH + 2])
    m.w2 = m.w[:, 0:EH].rearrange("p (n c) -> p n c", n=NCH)
    m.wqkv, m.wo = m.w[:, EH:EH + 3 * C], m.w[:, EH + 3 * C:2 * EH]
    m.bqk = m.w[:, 2 * EH:2 * EH + 2]
    m.bias = sb("bias", [P, 2 * C])
    m.bv, m.bo = m.bias[:, 0:C], m.bias[:, C:2 * C]
    m.bqs = sb("bqs", [C, 1])
    m.masks = sb("masks", [P, P + 2 * W], BF16)
    m.identb, m.band, m.bandT = m.masks[:, 0:P], m.masks[:, P:P + W], m.masks[:, P + W:P + 2 * W]
    m.mhalf = sb("mhalf", [P, 1])
    m.zero = sb("zero", [P, 6 * HALF], BF16)
    m.qs_all = sb("qs", [P, NBUF, H, P], BF16)
    m.ks_all = sb("ks", [P, NBUF, H, W], BF16)
    m.qs, m.ks = ([t[:, i] for i in range(NBUF)] for t in (m.qs_all, m.ks_all))

    def sem(name):
        return ctx.enter_context(nc.semaphore(name))

    m.in_x0 = sem("in_x0")
    m.in_x = sem("in_x")
    m.in_small = sem("in_small")
    m.in_w13 = sem("in_w13")
    m.in_w = sem("in_w")
    m.in_masks = sem("in_masks")
    m.in_ones = sem("in_ones")
    m.set = sem("set")
    m.zeroed = sem("zeroed")
    m.padded = sem("padded")
    m.psum = ctx.enter_context(nc.psum_tensor("psum", [P, 8, 512], F32))
    return m


def ffn_buffers(nc, ctx):
    b = Shared()

    def sb(name, shape, dt=F32):
        return ctx.enter_context(nc.sbuf_tensor(name, shape, dt))

    b.bnst = sb("bnst", [P, R, 6])
    b.mv = sb("mv", [P, R, 2])
    b.ve = sb("ve", [P, R, 1])
    b.nmean = sb("nmean", [P, R, 1])
    b.rstd = sb("rstd", [P, R, 1])
    b.shift = sb("shift", [P, R, 1])
    b.xn = sb("xn", [P, R, C])
    b.xnT = sb("xnT", [C, R, P])
    b.top = sb("top", [P, R, 8])
    b.topi = sb("topi", [P, R, 8], U32)
    b.nmax = sb("nmax", [P, R, 1])
    b.idx = sb("idx", [P, R, 2])
    b.hot1 = sb("hot1", [P, R, E])
    b.hot = sb("hot", [P, R, E])
    b.ex = sb("ex", [P, R, E])
    b.esum = sb("esum", [P, R, 1])
    b.rsum = sb("rsum", [P, R, 1])
    b.sc = sb("sc", [P, R, E])
    b.u = sb("u", [P, 2, EH])
    b.v = sb("v", [P, 2, EH])
    b.uv = sb("uv", [P, 2, EH])
    b.th = sb("th", [P, 2, EH])
    b.h = sb("h", [P, R, EH])
    b.hT = sb("hT", [P, R, NCH, P])
    b.bnst2 = sb("bnst2", [P, R, 6])
    b.mv2 = sb("mv2", [P, R, 2])
    b.ve2 = sb("ve2", [P, R, 1])
    b.nmean2 = sb("nmean2", [P, R, 1])
    b.rstd2 = sb("rstd2", [P, R, 1])
    b.shift2 = sb("shift2", [P, R, 1])
    b.xn2 = sb("xn2", [P, R, C])
    b.xn2T = sb("xn2T", [C, R, P])
    b.qk = sb("qk", [C, R, 2, P])
    b.rest = sb("rest", [C, R, 2, P])
    b.parts = sb("parts", [C, R, 3, 2, P], BF16)
    b.vaug = sb("vaug", [P, R, H, VD])
    return b


def ffn(nc, ctx, m, b, d, which):
    first = which == 0
    X, Y = (m.x[0], m.x[1]) if first else (m.x[2], m.x[3])
    def sem(name):
        return ctx.enter_context(nc.semaphore(f"{name}_{which}"))

    A, B, XT, LG, HT, YP0, YP1, QKV = (m.psum[:, i, :] for i in range(8))
    YP = (YP0, YP1)

    s = Shared()
    s.bnst = sem("s_bnst")
    s.stats = sem("s_stats")
    s.ve = sem("s_ve")
    s.nmean = sem("s_nmean")
    s.rstd = sem("s_rstd")
    s.shift = sem("s_shift")
    s.xn = sem("s_xn")
    s.xnT_ps = sem("s_xnT_ps")
    s.xnT = sem("s_xnT")
    s.logits = sem("s_logits")
    s.top = sem("s_top")
    s.topi = sem("s_topi")
    s.nmax = sem("s_nmax")
    s.idx = sem("s_idx")
    s.hot1 = sem("s_hot1")
    s.hot = sem("s_hot")
    s.ex = sem("s_ex")
    s.rsum = sem("s_rsum")
    s.sc = sem("s_sc")
    s.a = sem("s_a")
    s.b = sem("s_b")
    s.u = sem("s_u")
    s.v = sem("s_v")
    s.uv = sem("s_uv")
    s.th = sem("s_th")
    s.h = sem("s_h")
    s.hT_ps = sem("s_hT_ps")
    s.hT = sem("s_hT")
    s.y_ps = sem("s_y_ps")
    s.y = sem("s_y")
    s.bnst2 = sem("s_bnst2")
    s.stats2 = sem("s_stats2")
    s.ve2 = sem("s_ve2")
    s.nmean2 = sem("s_nmean2")
    s.rstd2 = sem("s_rstd2")
    s.shift2 = sem("s_shift2")
    s.xn2 = sem("s_xn2")
    s.xn2T_ps = sem("s_xn2T_ps")
    s.xn2T = sem("s_xn2T")
    s.qkv_ps = sem("s_qkv_ps")
    s.qk = sem("s_qk")
    s.part0 = sem("s_part0")
    s.rest = sem("s_rest")
    s.part1 = sem("s_part1")
    s.part2 = sem("s_part2")
    s.vaug = sem("s_vaug")
    s.set = sem("s_set")
    s.free, s.out = ([sem(f"s_{name}{i}") for i in range(R)] for name in ("free", "out"))
    if first:
        RANGE = (-3, NT + 6, 5, 2, R)
    else:
        RANGE = (-3, NT + 3, 5, 2, R)

    def vector(dve):
        if first:
            for i in range(R):
                nc.vector.memset(b.vaug[:, i], 1.0).then_inc(s.free[i], 16)
            dve.wait_ge(m.in_x0, 16)

        def body(t):
            n, k, k1, k3 = t.n, t.slot, (t + 1).slot, (t + 3).slot
            b1, b3, b5 = (t - 1).slot, (t - 3).slot, (t - 5).slot
            lg = LG[:, 0:E]
            scale = b.sc[:, k, :].unsqueeze(2).broadcast_to([P, E, FH])
            if first and (t + 3).at == 4:
                dve.wait_ge(m.in_x, 16)
            if first and (t + 1).at == 0:
                dve.wait_ge(m.in_small, 16)
            if first and t.at == 1:
                dve.wait_ge(m.in_w, 32)
                nc.vector.tensor_scalar(m.bqs[:], m.bqk[:, 0:1], HD ** -0.5, None, ALU.mult).then_inc(s.set, 1)
            if (t + 3).exists:
                if not first:
                    value = register(dve, n + 4)
                    dve.wait_ge(m.in_x0, 16)
                    dve.wait_ge(s.before.x2, value)
                nc.vector.bn_stats(b.bnst[:, k3, :], X[:, (t + 3).n, :]).then_inc(s.bnst, 1)
            if (t + 1).exists:
                value = register(dve, n + 2)
                dve.wait_ge(m.in_x0, 16)
                dve.wait_ge(s.logits, value)
                nc.vector.max(b.top[:, k1, :], lg).then_inc(s.top, 1)
            if (t + 3).exists:
                value = register(dve, n + 4)
                dve.wait_ge(m.in_x0, 16)
                dve.wait_ge(s.bnst, value)
                nc.vector.bn_aggr(b.mv[:, k3, :], b.bnst[:, k3, :]).then_inc(s.stats, 1)
            if (t + 1).exists:
                dve.wait_ge(s.top, n + 2)
                nc.vector.tensor_scalar(b.nmax[:, k1, :], b.top[:, k1, 0:1], -1.0, None, ALU.mult).then_inc(s.nmax, 1)
                nc.vector.max_index(b.topi[:, k1, :], b.top[:, k1, :], lg).then_inc(s.topi, 1)
            if (t - 3).exists:
                dve.wait_ge(s.y_ps, n - 2)
                nc.vector.scalar_tensor_tensor(Y[:, (t - 3).n, :], YP[(t - 3).at % 2][:, 0:C], 0.25,
                                               X[:, (t - 3).n, :], ALU.mult, ALU.add).then_inc(s.y, 1)
            if (t + 3).exists:
                dve.wait_ge(s.stats, n + 4)
                nc.vector.tensor_scalar(b.ve[:, k3, :], b.mv[:, k3, 1:2], EPS, None, ALU.add).then_inc(s.ve, 1)
                nc.vector.tensor_scalar(b.nmean[:, k3, :], b.mv[:, k3, 0:1], -1.0, None, ALU.mult
                                        ).then_inc(s.nmean, 1)
            if (t + 1).exists:
                dve.wait_ge(s.topi, n + 2)
                nc.vector.tensor_copy(b.idx[:, k1, :], b.topi[:, k1, 0:2]).then_inc(s.idx, 1)
            if first and (t - 3).exists:
                value = register(dve, n - 2)
                dve.wait_ge(m.in_x0, 16)
                dve.wait_ge(s.y, value)
                nc.vector.bn_stats(b.bnst2[:, b3, :], Y[:, (t - 3).n, :]).then_inc(s.bnst2, 1)
            if (t + 1).exists:
                dve.wait_ge(s.idx, n + 2)
                nc.vector.tensor_scalar(b.hot1[:, k1, :], m.iota[:], b.idx[:, k1, 0:1], None,
                                        ALU.is_equal).then_inc(s.hot1, 1)
            if first and (t - 3).exists:
                value = register(dve, n - 2)
                dve.wait_ge(m.in_x0, 16)
                dve.wait_ge(s.bnst2, value)
                nc.vector.bn_aggr(b.mv2[:, b3, :], b.bnst2[:, b3, :]).then_inc(s.stats2, 1)
            if (t - 1).exists:
                dve.wait_ge(s.th, n)
                dve.wait_ge(s.uv, n)
                nc.vector.scalar_tensor_tensor(b.h[:, b1, :], b.th[:, b1 % 2, :], 1.0, b.uv[:, b1 % 2, :],
                                               ALU.add, ALU.mult).then_inc(s.h, 1)
            if first and (t - 3).exists:
                dve.wait_ge(s.stats2, n - 2)
                nc.vector.tensor_scalar(b.ve2[:, b3, :], b.mv2[:, b3, 1:2], EPS, None, ALU.add).then_inc(s.ve2, 1)
                nc.vector.tensor_scalar(b.nmean2[:, b3, :], b.mv2[:, b3, 0:1], -1.0, None, ALU.mult
                                        ).then_inc(s.nmean2, 1)
            if t.exists:
                dve.wait_ge(s.a, n + 1)
                dve.wait_ge(s.sc, n + 1)
                nc.vector.tensor_tensor(b.u[:, k % 2, :].rearrange("p (e f) -> p e f", e=E),
                                        A.rearrange("p (e f) -> p e f", e=E), scale, ALU.mult).then_inc(s.u, 1)
            if (t + 1).exists:
                dve.wait_ge(s.hot1, n + 2)
                nc.vector.scalar_tensor_tensor(b.hot[:, k1, :], m.iota[:], b.idx[:, k1, 1:2], b.hot1[:, k1, :],
                                               ALU.is_equal, ALU.add).then_inc(s.hot, 1)
                dve.wait_ge(s.ex, n + 2)
                nc.vector.reciprocal(b.rsum[:, k1, :], b.esum[:, k1, :]).then_inc(s.rsum, 1)
            if first and (t - 5).exists:
                dve.wait_ge(s.qkv_ps, n - 4)
                dve.wait_ge(s.qk, n - 4)
                dve.wait_ge(s.free[b5], 16 * NSAVE * (t - 5).round + 16)
                nc.vector.tensor_tensor(b.vaug[:, b5, :, 0:HD],
                                        QKV[:, 2 * P:3 * P].rearrange("p (h d) -> p h d", h=H),
                                        m.bv[:].rearrange("p (h d) -> p h d", h=H), ALU.add).then_inc(s.vaug, 1)
            if t.exists:
                dve.wait_ge(s.b, n + 1)
                nc.vector.tensor_tensor(b.v[:, k % 2, :].rearrange("p (e f) -> p e f", e=E),
                                        B.rearrange("p (e f) -> p e f", e=E), scale, ALU.mult).then_inc(s.v, 1)
            if (t + 1).exists:
                dve.wait_ge(s.rsum, n + 2)
                dve.wait_ge(s.hot, n + 2)
                nc.vector.scalar_tensor_tensor(b.sc[:, k1, :], b.ex[:, k1, :], b.rsum[:, k1, :], b.hot[:, k1, :],
                                               ALU.mult, ALU.mult).then_inc(s.sc, 1)

        run_tiles(dve, *RANGE, body)

    def gpsimd(pool):
        def body(t):
            n, k, k3 = t.n, t.slot, (t + 3).slot
            b3, b5 = (t - 3).slot, (t - 5).slot
            if (t + 3).exists:
                pool.wait_ge(s.ve, n + 4)
                nc.gpsimd.tensor_tensor(b.rstd[:, k3, :], b.ve[:, k3, :], m.mhalf[:], ALU.pow).then_inc(s.rstd, 1)
                pool.wait_ge(s.rstd, n + 4)
                pool.wait_ge(s.nmean, n + 4)
                nc.gpsimd.tensor_tensor(b.shift[:, k3, :], b.nmean[:, k3, :], b.rstd[:, k3, :], ALU.mult
                                        ).then_inc(s.shift, 1)
            if first and (t - 5).exists:
                pool.wait_ge(s.part0, n - 4)
                nc.gpsimd.tensor_tensor(b.rest[:, b5], b.qk[:, b5], b.parts[:, b5, 0], ALU.subtract
                                        ).then_inc(s.rest, 1)
            if first and (t - 3).exists:
                pool.wait_ge(s.ve2, n - 2)
                nc.gpsimd.tensor_tensor(b.rstd2[:, b3, :], b.ve2[:, b3, :], m.mhalf[:], ALU.pow).then_inc(s.rstd2, 1)
                pool.wait_ge(s.rstd2, n - 2)
                pool.wait_ge(s.nmean2, n - 2)
                nc.gpsimd.tensor_tensor(b.shift2[:, b3, :], b.nmean2[:, b3, :], b.rstd2[:, b3, :], ALU.mult
                                        ).then_inc(s.shift2, 1)
            if t.exists:
                pool.wait_ge(s.v, n + 1)
                nc.gpsimd.tensor_tensor(b.uv[:, k % 2, :], b.u[:, k % 2, :], b.v[:, k % 2, :], ALU.mult).then_inc(s.uv, 1)
            if first and (t - 5).exists:
                pool.wait_ge(s.part1, n - 4)
                nc.gpsimd.tensor_tensor(b.parts[:, b5, 2], b.rest[:, b5], b.parts[:, b5, 1],
                                        ALU.subtract).then_inc(s.part2, 1)
            if first and t.at == NT - 2:
                nc.gpsimd.memset(m.qs_all[:].bitcast(F32), 0.0).then_inc(m.zeroed, 1)
            if first and t.at == NT - 1:
                nc.gpsimd.memset(m.ks_all[:].bitcast(F32), 0.0).then_inc(m.zeroed, 1)

        run_tiles(pool, *RANGE, body)

    def scalar(act):
        def body(t):
            n, k = t.n, t.slot
            if first and t.at == 2:
                act.wait_ge(s.set, 1)
            if first and (t - 5).exists:
                b5 = (t - 5).slot
                act.wait_ge(s.qkv_ps, n - 4)
                nc.scalar.activation(b.qk[:, b5, 0, :], QKV[:, 0:P], ACT.Identity, bias=m.bqs[:], scale=HD ** -0.5)
                nc.scalar.activation(b.qk[:, b5, 1, :], QKV[:, P:2 * P], ACT.Identity,
                                     bias=m.bqk[:, 1:2]).then_inc(s.qk, 1)
            if (t - 2).exists:
                b2 = (t - 2).slot
                act.wait_ge(s.hT_ps, n - 1)
                nc.scalar.activation(b.hT[:, b2].rearrange("p n q -> p (n q)"), HT, ACT.Copy).then_inc(s.hT, 1)
            if first and (t - 4).exists:
                b4 = (t - 4).slot
                act.wait_ge(s.xn2T_ps, n - 3)
                nc.scalar.activation(b.xn2T[:, b4, :], XT[:, P:2 * P], ACT.Copy).then_inc(s.xn2T, 1)
            if (t + 1).exists:
                k1 = (t + 1).slot
                act.wait_ge(s.nmax, n + 2)
                act.wait_ge(s.topi, n + 2)
                nc.scalar.activation(b.ex[:, k1, :], LG[:, 0:E], ACT.Exp, bias=b.nmax[:, k1, :],
                                     accum_out=b.esum[:, k1, :]).then_inc(s.ex, 1)
            if first and (t - 5).exists:
                act.wait_ge(s.qk, n - 4)
                act.wait_ge(s.free[b5], 16 * NSAVE * (t - 5).round + 16)
                nc.scalar.activation(b.parts[:, b5, 0], b.qk[:, b5], ACT.Copy).then_inc(s.part0, 1)
            if (t + 2).exists:
                k2 = (t + 2).slot
                act.wait_ge(s.xnT_ps, n + 3)
                nc.scalar.activation(b.xnT[:, k2, :], XT[:, 0:P], ACT.Copy).then_inc(s.xnT, 1)
            if t.exists:
                act.wait_ge(s.u, n + 1)
                nc.scalar.activation(b.th[:, k % 2, :], b.u[:, k % 2, :], ACT.Tanh, scale=0.5).then_inc(s.th, 1)
            if (t + 3).exists:
                k3 = (t + 3).slot
                act.wait_ge(s.shift, n + 4)
                nc.scalar.activation(b.xn[:, k3, :], X[:, (t + 3).n, :], ACT.Identity, bias=b.shift[:, k3, :],
                                     scale=b.rstd[:, k3, :]).then_inc(s.xn, 1)
            if first and (t - 5).exists:
                act.wait_ge(s.rest, n - 4)
                nc.scalar.activation(b.parts[:, b5, 1], b.rest[:, b5], ACT.Copy).then_inc(s.part1, 1)
            if first and (t - 3).exists:
                b3 = (t - 3).slot
                act.wait_ge(s.shift2, n - 2)
                nc.scalar.activation(b.xn2[:, b3, :], Y[:, (t - 3).n, :], ACT.Identity, bias=b.shift2[:, b3, :],
                                     scale=b.rstd2[:, b3, :]).then_inc(s.xn2, 1)

        run_tiles(act, *RANGE, body)

    def tensor(pe):
        if first:
            pe.wait_ge(m.in_small, 16)
        else:
            pe.wait_ge(s.before.max, 2 * PAIRS * NT)
            pe.wait_ge(s.before.exp, PAIRS * NT)
            pe.wait_ge(s.before.nmr, NT)
            pe.wait_ge(s.before.x2, NT)

        def body(t):
            n, k = t.n, t.slot
            if first and t.at == 0:
                pe.wait_ge(m.in_w13, 16)
            if first and t.at == 2:
                pe.wait_ge(m.in_w, 32)
            if (t - 2).exists:
                b2 = (t - 2).slot
                pe.wait_ge(s.h, n - 1)
                for c in range(NCH):
                    last = nc.tensor.transpose(HT[:, c * P:(c + 1) * P], b.h[:, b2, c * P:(c + 1) * P], m.ident[:])
                last.then_inc(s.hT_ps, 1)
            if first and (t - 4).exists:
                b4 = (t - 4).slot
                pe.wait_ge(s.xn2, n - 3)
                pe.wait_ge(s.xnT, min(n + 2, NT) if isinstance(n, int) else n + 2)
                nc.tensor.transpose(XT[:, P:2 * P], b.xn2[:, b4, :], m.ident[:]).then_inc(s.xn2T_ps, 1)
            if t.exists:
                pe.wait_ge(s.xnT, n + 1)
                pe.wait_ge(s.u, count(n))
                nc.tensor.matmul(A, b.xnT[:, k, :], m.w1[:], start=True, stop=True).then_inc(s.a, 1)
            if (t + 2).exists:
                pe.wait_ge(s.xn, n + 3)
                pe.wait_ge(s.xnT, count(n + 2))
                if first:
                    pe.wait_ge(s.xn2T, count(n - 3))
                nc.tensor.transpose(XT[:, 0:P], b.xn[:, (t + 2).slot, :], m.ident[:]).then_inc(s.xnT_ps, 1)
            if t.exists:
                pe.wait_ge(s.v, count(n))
                nc.tensor.matmul(B, b.xnT[:, k, :], m.w3[:], start=True, stop=True).then_inc(s.b, 1)
            if (t - 2).exists:
                pe.wait_ge(s.hT, n - 1)
                pe.wait_ge(s.y, count(n - 3))
                for c in range(NCH):
                    last = nc.tensor.matmul(YP[t.at % 2][:, 0:C], b.hT[:, b2, c, :], m.w2[:, c, :],
                                            start=(c == 0), stop=(c == NCH - 1))
                last.then_inc(s.y_ps, 1)
            if first and (t - 4).exists:
                pe.wait_ge(s.xn2T, n - 3)
                pe.wait_ge(s.vaug, count(n - 4))
                for c in range(2):
                    nc.tensor.matmul(QKV[:, c * P:(c + 1) * P], m.wqkv[:, c * C:(c + 1) * C], b.xn2T[:, b4, :],
                                     start=True, stop=True)
                nc.tensor.matmul(QKV[:, 2 * P:3 * P], b.xn2T[:, b4, :], m.wqkv[:, 2 * C:3 * C],
                                 start=True, stop=True).then_inc(s.qkv_ps, 1)
            if (t + 2).exists:
                pe.wait_ge(s.xnT, n + 3)
                pe.wait_ge(s.ex, count(n + 2))
                nc.tensor.matmul(LG[:, 0:E], b.xnT[:, (t + 2).slot, :], m.gate[:],
                                 start=True, stop=True).then_inc(s.logits, 1)

        run_tiles(pe, *RANGE, body)

    def sync(sp):
        if first:
            def body(t):
                at = HALF + t.n * P
                if t.at == NT - R:
                    for i in range(R):
                        sp.wait_ge(s.free[i], 16 * NSAVE * (NT // R - 1) + 16)
                    sp.wait_ge(m.padded, 80)
                    sp.wait_ge(m.zeroed, 2)
                    sp.dma_start(m.qs_all[R_DATA:R_VALID],
                                 d.ones[0:1, 0:NBUF * H * P].rearrange("a (n h q) -> a n h q", n=NBUF, h=H)
                                 ).then_inc(m.in_ones, 16)
                    sp.dma_start(m.ks_all[R_VALID:R_ALL], d.ones.rearrange("a (n h q) -> a n h q", n=NBUF, h=H)
                                 ).then_inc(m.in_ones, 16)
                    for i in range(AHEAD):
                        s.after.load(sp, Tile(0, i, NBUF))
                sp.wait_ge(s.part2, t.n + 1)
                row = 0
                for kpart, nq in GROUPS:
                    rows = slice(row * HD, (row + nq) * HD)
                    row += nq
                    sp.dma_start(d.scrk[rows, :, bass.ds(at, P)].rearrange("(p d) h t -> (d h) p t", p=nq),
                                 b.parts[:, t.slot, kpart, 1, :].unsqueeze(1).broadcast_to([C, nq, P])
                                 ).then_inc(s.free[t.slot], 16)
                    sp.dma_start(d.scrq[rows, :, bass.ds(t.n * P, P)].rearrange("(p d) h t -> (d h) p t", p=nq),
                                 b.parts[:, t.slot, 0:nq, 0, :]).then_inc(s.free[t.slot], 16)
                sp.wait_ge(s.vaug, t.n + 1)
                sp.dma_start(d.scrv[bass.ds(at, P), :],
                             b.vaug[:, t.slot].rearrange("p h d -> p (h d)")).then_inc(s.free[t.slot], 16)

            run_tiles(sp, 0, NT, 0, NT // R - 1, R, body)
        else:
            def body(t):
                sp.wait_ge(s.y, t.n + 1)
                sp.dma_start(d.out[bass.ds(t.n * P, P), :], Y[:, t.n, :]).then_inc(s.out[t.slot], 16)

            run_tiles(sp, 0, NT, 0, NT // R, R, body)
            for i in range(R):
                sp.wait_ge(s.out[i], 16 * NT // R)

    s.vector, s.gpsimd, s.scalar, s.tensor, s.sync = vector, gpsimd, scalar, tensor, sync
    return s


def attention(nc, ctx, m, d, before):
    def sb(name, shape, dt=F32):
        return ctx.enter_context(nc.sbuf_tensor(name, shape, dt))

    def sem(name):
        return ctx.enter_context(nc.semaphore("s_" + name))

    qs, ks = m.qs, m.ks
    vs = [sb(f"vs{i}", [P, 2, H * VD]) for i in range(NBUF)]
    mx = [sb(f"mx{i}", [P, H]) for i in range(NBUF)]
    junk = sb("junk", [P, 4, W], BF16)
    nmr = [sb(f"nmr{i}", [H, P]) for i in range(NBUF)]
    nmp = [sb(f"nmp{i}", [H, 3, P], BF16) for i in range(NBUF)]
    pr = [sb(f"pr{i}", [P, 2, 2, P]) for i in range(4)]
    ot = sb("ot", [P, 4, P])
    rs = sb("rs", [P, H])
    o = sb("o", [P, C])
    oT = sb("oT", [C, P])

    SA = [m.psum[:, i, :] for i in range(2)]
    SB = [m.psum[:, 2 + i, :] for i in range(2)]
    OT, OX, NM, PJ = (m.psum[:, i, :] for i in range(4, 8))

    s = Shared()
    s.max = sem("t_max")
    s.mxT_ps = sem("t_mxT_ps")
    s.nmp0 = sem("t_nmp0")
    s.nmr = sem("t_nmr")
    s.nmp1 = sem("t_nmp1")
    s.nmp2 = sem("t_nmp2")
    s.x1b = sem("t_x1b")
    s.sa = sem("t_sa")
    s.sb = sem("t_sb")
    s.exp = sem("t_exp")
    s.pv = sem("t_pv")
    s.ot = sem("t_ot")
    s.ox = sem("t_ox")
    s.rs = sem("t_rs")
    s.o = sem("t_o")
    s.oT_ps = sem("t_oT_ps")
    s.oT = sem("t_oT")
    s.pj = sem("t_pj")
    s.x2 = sem("t_x2")
    s.q, s.k, s.v, s.nm_in = ([sem(f"t_{name}{i}") for i in range(NBUF)] for name in ("q", "k", "v", "nm_in"))
    RANGE = (0, NT + 4, 4, 3, NBUF)

    def back(t, i, lag):
        return t - (lag - i + PAIRS - 1) // PAIRS, (i - lag) % PAIRS

    def load(sp, t):
        n, k = t.n, t.slot
        sp.wait_ge(s.sb, count(PAIRS * (n - NBUF + 1)))
        sp.dma_start(ks[k][0:R_VALID, :, :], d.scrk[:, :, bass.ds(n * P, W)]).then_inc(s.k[k], 16)
        sp.dma_start(qs[k][0:R_DATA, :, :], d.scrq[:, :, bass.ds(n * P, P)]).then_inc(s.q[k], 16)
        sp.wait_ge(s.pv, count(4 * (n - NBUF + 1)))
        sp.dma_start(vs[k][:], d.scrv[bass.ds(n * P, W), :].rearrange("(s p) c -> p s c", p=P)
                     ).then_inc(s.v[k], 16)

    s.load = load

    def sync(sp):
        def body(t):
            if (t + 1).exists and (t + 1).at >= AHEAD:
                load(sp, t + 1)
            if t.at == 2:
                for i in range(R):
                    sp.wait_ge(before.free[i], 16 * NSAVE * NT // R + 16)
            if (t - 1).exists:
                k = (t - 1).slot
                for p, part in enumerate((s.nmp0, s.nmp1, s.nmp2)):
                    sp.wait_ge(part, t.n)
                    sp.dma_start(qs[k][R_VALID + p:R_VALID + p + 1, :, :], nmp[k][:, p, :]
                                 ).then_inc(s.nm_in[k], 16)

        run_tiles(sp, 0, NT + 1, 3, 3, NBUF, body)

    def gpsimd(pool):
        pool.wait_ge(m.in_w, 32)
        pool.wait_ge(before.y, NT)
        def body(t):
            nc.gpsimd.tensor_tensor(m.x1b[:, t.n, :], m.x[1][:, t.n, :], m.bo[:], ALU.add).then_inc(s.x1b, 1)

        run_tiles(pool, 0, NT, 0, NT // NBUF, NBUF, body)

    def vector(dve):
        dve.wait_ge(m.in_masks, 16)

        def body(t):
            n, k, j = t.n, t.slot, (t - 1).slot
            for i in range(PAIRS):
                if t.exists:
                    value = register(dve, PAIRS * n + i + 1)
                    dve.wait_ge(m.in_x0, 16)
                    dve.wait_ge(s.sa, value)
                    for e in range(2):
                        nc.vector.tensor_tensor_reduce(
                            out=junk[:, (2 * i + e) % 4, :], in0=SA[i % 2][:, e * W:(e + 1) * W], in1=m.band[:],
                            scale=1.0, scalar=FLOOR, op0=ALU.add, op1=ALU.max,
                            accum_out=mx[k][:, 2 * i + e:2 * i + e + 1]).then_inc(s.max, 1)
                if i == 1 and (t - 1).exists:
                    dve.wait_ge(s.mxT_ps, n)
                    dve.wait_ge(s.nm_in[(t - 4).slot], count(48 * (t - 4).round + 48))
                    nc.vector.tensor_scalar(nmp[j][:, 0, :], NM[0:H, 0:P], -1.0, None, ALU.mult
                                            ).then_inc(s.nmp0, 1)
                if i == 2 and (t - 1).exists:
                    dve.wait_ge(s.nmp0, n)
                    nc.vector.scalar_tensor_tensor(nmr[j][:], NM[0:H, 0:P], -1.0, nmp[j][:, 0, :],
                                                   ALU.mult, ALU.subtract).then_inc(s.nmr, 1)
                if i == 3 and (t - 1).exists:
                    dve.wait_ge(s.nmr, n)
                    nc.vector.tensor_copy(nmp[j][:, 1, :], nmr[j][:]).then_inc(s.nmp1, 1)
                if i == 4 and (t - 1).exists:
                    dve.wait_ge(s.nmp1, n)
                    nc.vector.tensor_tensor(nmp[j][:, 2, :], nmr[j][:], nmp[j][:, 1, :], ALU.subtract
                                            ).then_inc(s.nmp2, 1)
                if i == 4 and (t - 3).exists:
                    dve.wait_ge(s.ox, n - 2)
                    nc.vector.reciprocal(rs[:].rearrange("p (g j) -> p g j", g=4),
                                         OX.rearrange("p (g j c) -> p g j c", g=4, j=4)[:, :, :, HD]
                                         ).then_inc(s.rs, 1)
                if i == 5 and (t - 3).exists:
                    dve.wait_ge(s.rs, n - 2)
                    nc.vector.tensor_tensor(o[:].rearrange("p (h d) -> p h d", h=H),
                                            OX.rearrange("p (h c) -> p h c", h=H)[:, :, 0:HD],
                                            rs[:].unsqueeze(2).broadcast_to([P, H, HD]), ALU.mult
                                            ).then_inc(s.o, 1)
                if i == 0 and (t - 4).exists:
                    dve.wait_ge(s.pj, n - 3)
                    dve.wait_ge(s.x1b, n - 3)
                    nc.vector.tensor_tensor(m.x[2][:, (t - 4).n, :], PJ[:, P:P + C], m.x1b[:, (t - 4).n, :],
                                            ALU.add).then_inc(s.x2, 1)

        run_tiles(dve, *RANGE, body)

    def scalar(act):
        def body(t):
            for i in range(PAIRS):
                if i == 2 and (t - 3).exists:
                    act.wait_ge(s.pv, 4 * (t - 2).n)
                    nc.scalar.activation(ot[:].rearrange("p g q -> p (g q)"), OT, ACT.Copy).then_inc(s.ot, 1)
                if i == 7 and (t - 3).exists:
                    act.wait_ge(s.oT_ps, (t - 2).n)
                    nc.scalar.activation(oT[:], PJ[:, 0:P], ACT.Copy).then_inc(s.oT, 1)
                tb, pb = back(t, i, LAG)
                if tb.exists:
                    act.wait_ge(s.sb, PAIRS * tb.n + pb + 1)
                    act.wait_ge(s.pv, count(4 * tb.n + pb // 2 - 1))
                    nc.scalar.activation(pr[pb % 4][:].rearrange("p h s q -> p (h s q)"), SB[pb % 2],
                                         ACT.Exp).then_inc(s.exp, 1)

        run_tiles(act, *RANGE, body)

    def tensor(pe):
        pe.wait_ge(m.in_masks, 16)
        pe.wait_ge(m.in_ones, 32)
        pe.wait_ge(before.v, NT)
        pe.wait_ge(before.u, NT)
        pe.wait_ge(before.xn2T, NT)
        pe.wait_ge(before.topi, NT)
        pe.wait_ge(before.ex, NT)
        pe.wait_ge(before.hT, NT)
        pe.wait_ge(before.y, NT)
        pe.wait_ge(before.qk, NT)
        pe.wait_ge(before.vaug, NT)

        def body(t):
            n, k = t.n, t.slot
            for i in range(PAIRS):
                if t.exists:
                    if i == 0:
                        pe.wait_ge(s.q[k], 16 * (t.round + 1))
                        pe.wait_ge(s.k[k], 16 * (t.round + 1))
                    pe.wait_ge(s.max, count(2 * (PAIRS * n + i - 1)))
                    for e in range(2):
                        last = nc.tensor.matmul(SA[i % 2][:, e * W:(e + 1) * W], qs[k][0:R_VALID, 2 * i + e, :],
                                                ks[k][0:R_VALID, 2 * i + e, :], start=True, stop=True)
                    last.then_inc(s.sa, 1)
                if i == 1 and (t - 1).exists:
                    pe.wait_ge(s.max, 2 * PAIRS * n)
                    pe.wait_ge(s.nmr, count(n - 1))
                    nc.tensor.transpose(NM[0:H, 0:P], mx[(t - 1).slot][:], m.ident[:]).then_inc(s.mxT_ps, 1)
                tb, pb = back(t, i, LAG)
                if tb.exists:
                    kb = tb.slot
                    if pb == 0:
                        pe.wait_ge(s.nm_in[kb], 48 * (tb.round + 1))
                    pe.wait_ge(s.exp, count(PAIRS * tb.n + pb - 1))
                    bank = SB[pb % 2]
                    nc.tensor.matmul(bank.rearrange("p (h k) -> p h k", h=2), m.identb[:],
                                     m.bandT[:].unsqueeze(1).broadcast_to([P, 2, W]), start=True, stop=False)
                    for e in range(2):
                        for half in range(2):
                            at = (2 * e + half) * P
                            last = nc.tensor.matmul(bank[:, at:at + P],
                                                    ks[kb][:, 2 * pb + e, half * P:(half + 1) * P],
                                                    qs[kb][:, 2 * pb + e, :], start=False,
                                                    stop=(e == 1 and half == 1))
                    last.then_inc(s.sb, 1)
                tv, pv = back(t, i, LAG + 2)
                if pv % 2 == 1 and tv.exists:
                    kv, g = tv.slot, pv // 2
                    pe.wait_ge(s.exp, PAIRS * tv.n + pv + 1)
                    if g == 0:
                        pe.wait_ge(s.v[kv], 16 * (tv.round + 1))
                        pe.wait_ge(s.ot, count(tv.n))
                    for half in range(2):
                        for j in range(4):
                            hh = 4 * g + j
                            last = nc.tensor.matmul(OT[32 * j:32 * j + VD, g * P:(g + 1) * P],
                                                    vs[kv][:, half, hh * VD:(hh + 1) * VD],
                                                    pr[(2 * g + j // 2) % 4][:, j % 2, half, :],
                                                    start=(half == 0), stop=(half == 1))
                    last.then_inc(s.pv, 1)
                if i == 3 and (t - 3).exists:
                    pe.wait_ge(s.ot, n - 2)
                    pe.wait_ge(s.o, n - 3)
                    for g in range(4):
                        last = nc.tensor.transpose(OX[:, g * P:(g + 1) * P], ot[:, g, :], m.ident[:])
                    last.then_inc(s.ox, 1)
                if i == 6 and (t - 3).exists:
                    pe.wait_ge(s.o, n - 2)
                    pe.wait_ge(s.x2, n - 3)
                    nc.tensor.transpose(PJ[:, 0:P], o[:], m.ident[:]).then_inc(s.oT_ps, 1)
                if i == 7 and (t - 3).exists:
                    pe.wait_ge(s.oT, n - 2)
                    nc.tensor.matmul(PJ[:, P:P + C], oT[:], m.wo[:], start=True, stop=True).then_inc(s.pj, 1)

        run_tiles(pe, *RANGE, body)

    s.vector, s.gpsimd, s.scalar, s.tensor, s.sync = vector, gpsimd, scalar, tensor, sync
    return s


def load(sp, m, d):
    xv = d.x.rearrange("(t p) c -> p t c", p=P)
    sp.dma_start(m.x[0][:, 0:4, :], xv[:, 0:4, :]).then_inc(m.in_x0, 16)
    sp.dma_start(m.small[:], d.small).then_inc(m.in_small, 16)
    sp.dma_start(m.w13[:], d.w13).then_inc(m.in_w13, 16)
    sp.dma_start(m.x[0][:, 4:NT, :], xv[:, 4:NT, :]).then_inc(m.in_x, 16)
    sp.dma_start(m.w[:], d.w).then_inc(m.in_w, 16)
    sp.dma_start(m.bias[:], d.bias.partition_broadcast(P)).then_inc(m.in_w, 16)
    sp.dma_start(m.masks[:], d.masks).then_inc(m.in_masks, 16)
    sp.wait_ge(m.set, 2)
    for at in (0, T + HALF):
        sp.dma_start(d.scrk[0:R_DATA, :, at:at + HALF].rearrange("r h t -> (r h) t")
                     .rearrange("(p k) t -> p k t", k=6),
                     m.zero[:, :].rearrange("p (k t) -> p k t", k=6)).then_inc(m.padded, 16)
        sp.dma_start(d.scrv[at:at + HALF, :],
                     m.zero[0:HALF, 0:2 * H * VD].bitcast(F32)).then_inc(m.padded, 16)
    sp.dma_start(d.scrk[R_DATA:R_VALID, :, :], d.valid).then_inc(m.padded, 16)


def build(nc, d):
    with ExitStack() as ctx:
        m = allocate(nc, ctx)
        b = ffn_buffers(nc, ctx)
        first = ffn(nc, ctx, m, b, d, 0)
        att = attention(nc, ctx, m, d, first)
        second = ffn(nc, ctx, m, b, d, 1)
        first.after, second.before = att, att
        block = ctx.enter_context(nc.Block())

        @block.sync
        def _(sp):
            load(sp, m, d)
            first.sync(sp)
            att.sync(sp)
            second.sync(sp)

        @block.gpsimd
        def _(pool):
            pool.wait_ge(m.set, 2)
            first.gpsimd(pool)
            att.gpsimd(pool)
            second.gpsimd(pool)

        @block.vector
        def _(dve):
            nc.vector.memset(m.zero[:], 0.0).then_inc(m.set, 1)
            nc.vector.memset(m.mhalf[:], -0.5).then_inc(m.set, 1)
            first.vector(dve)
            att.vector(dve)
            second.vector(dve)

        @block.scalar
        def _(act):
            first.scalar(act)
            att.scalar(act)
            second.scalar(act)

        @block.tensor
        def _(pe):
            first.tensor(pe)
            att.tensor(pe)
            second.tensor(pe)


def kernel(L0_attn_x, L0_attn_in_proj_w, L0_attn_in_proj_b, L0_attn_out_w, L0_attn_out_b, L0_ffn_gate_w, L0_ffn_w1,
           L0_ffn_w2, L0_ffn_w3):
    import concourse.bacc as _bacc
    import ml_dtypes
    from concourse.bass_utils import run_bass_kernel_spmd as _run

    def flat(a):
        return np.ascontiguousarray(a)

    i, c = np.arange(P)[:, None], np.arange(W)[None, :]
    band = np.where((c >= i) & (c <= i + 2 * HALF), 0.0, BIG).astype(ml_dtypes.bfloat16)
    q = c % P
    bandT = np.where(np.where(c < P, q <= i, q >= i), 0.0, BIG).astype(ml_dtypes.bfloat16)
    exists = np.full((1, H, TP), BIG)
    exists[:, :, HALF:HALF + T] = 0.0
    w1, w3 = (np.transpose(w, (1, 0, 2)).reshape(C, EH) for w in (L0_ffn_w1, L0_ffn_w3))
    w2 = np.transpose(np.reshape(L0_ffn_w2, (NCH, P, C)), (1, 0, 2)).reshape(P, EH)
    wqk = np.transpose(np.reshape(L0_attn_in_proj_w[0:2 * C], (2, H, HD, C)), (3, 0, 2, 1)).reshape(C, 2 * C)
    wv, wo = np.transpose(L0_attn_in_proj_w[2 * C:]), np.transpose(L0_attn_out_w)
    bqk = np.transpose(np.reshape(L0_attn_in_proj_b[0:2 * C], (2, H, HD)), (2, 1, 0)).reshape(C, 2)
    iota = np.broadcast_to(np.arange(E, dtype=np.float32), (P, E))
    arrays = {
        "x": flat(L0_attn_x).reshape(T, C),
        "small": np.concatenate([L0_ffn_gate_w, iota, np.eye(P, dtype=np.float32)], axis=1),
        "w13": np.concatenate([w1, w3], axis=1),
        "w": np.concatenate([w2, wqk, wv, wo, bqk], axis=1),
        "bias": np.concatenate([L0_attn_in_proj_b[2 * C:], L0_attn_out_b]),
        "masks": np.concatenate([np.eye(P).astype(ml_dtypes.bfloat16), band, bandT], axis=1),
        "valid": exists.astype(ml_dtypes.bfloat16),
        "ones": np.ones((3, NBUF * H * W), ml_dtypes.bfloat16),
    }
    nc = _bacc.Bacc("TRN2", target_bir_lowering=False, num_devices=1)

    def dram(name):
        a = arrays[name]
        return nc.dram_tensor(f"in_{name}", a.shape, mybir.dt.from_np(a.dtype), kind="ExternalInput").ap()

    d = Shared()
    d.x = dram("x")
    d.small = dram("small")
    d.w13 = dram("w13")
    d.w = dram("w")
    d.bias = dram("bias")
    d.masks = dram("masks")
    d.valid = dram("valid")
    d.ones = dram("ones")
    d.scrk = nc.dram_tensor("scrk", (R_VALID, H, TP), BF16, kind="Internal").ap()
    d.scrq = nc.dram_tensor("scrq", (R_DATA, H, T), BF16, kind="Internal").ap()
    d.scrv = nc.dram_tensor("scrv", (TP, H * VD), F32, kind="Internal").ap()
    d.out = nc.dram_tensor("out_0", (T, C), F32, kind="ExternalOutput").ap()
    build(nc, d)
    r = _run(nc, [{f"in_{name}": a for name, a in arrays.items()}], core_ids=[0])
    return r.results[0]["out_0"].reshape(1, T, C)
```

```python
from contextlib import ExitStack

import numpy as np

import concourse.bass as bass
from concourse import mybir

F32 = mybir.dt.float32
BF16 = mybir.dt.bfloat16
U32 = mybir.dt.uint32
ALU = mybir.AluOpType
ACT = mybir.ActivationFunctionType

T, C = 2048, 128
P = 128
NT = T // P
H, HD = 16, 8
E, FH = 8, 64
EH = E * FH
NCH = EH // P
HALF = 64
TP = T + 2 * HALF
W = 2 * P
VD = HD + 1
PAIRS = H // 2
GROUPS = ((0, 3), (1, 2), (2, 1))
NPROD = 6
NSAVE = 2 * len(GROUPS) + 1
R = 4
R_DATA = NPROD * HD
R_VALID = R_DATA + 1
R_ALL = R_VALID + 3
FLOOR = -3.0e38
BIG = -1.0e38
EPS = 1e-5
LAG = 16
AHEAD = 3
NBUF = 4
BETWEEN = {(NT, 1): -3, (NT, 4): -2, (NT, 7): -1, (NT + 1, 3): 0, (NT + 1, 7): 1, (NT + 2, 2): 2, (NT + 2, 6): 3}


class Shared:
    pass


class Tile:

    def __init__(self, i, at, ring):
        self.i, self.at, self.ring = i, at, ring

    def __add__(self, n):
        return Tile(self.i, self.at + n, self.ring)

    def __sub__(self, n):
        return Tile(self.i, self.at - n, self.ring)

    @property
    def n(self):
        return self.i * self.ring + self.at

    @property
    def slot(self):
        return self.at % self.ring

    @property
    def round(self):
        return self.i + self.at // self.ring

    @property
    def exists(self):
        return not isinstance(self.i, int) or 0 <= self.at < NT


def count(value):
    return max(value, 0) if isinstance(value, int) else value


def register(engine, value):
    return value if isinstance(value, int) else engine.to_reg(value)


def run_tiles(engine, first, last, lo, rounds, ring, body):
    for at in range(first, lo):
        body(engine, Tile(0, at, ring))
    with engine.Fori(0, rounds) as i:
        for k in range(ring):
            body(engine, Tile(i, lo + k, ring))
    for at in range(lo + ring * rounds, last):
        body(engine, Tile(0, at, ring))


def allocate(nc, ctx):
    m = Shared()

    def sb(name, shape, dt=F32):
        return ctx.enter_context(nc.sbuf_tensor(name, shape, dt))

    m.x = [sb(f"x{i}", [P, NT, C]) for i in range(4)]
    m.x1b = sb("x1b", [P, NT, C])
    m.small = sb("small", [C, 2 * E + P])
    m.gate, m.iota, m.ident = m.small[:, 0:E], m.small[:, E:2 * E], m.small[:, 2 * E:2 * E + P]
    m.w13 = sb("w13", [C, 2 * EH])
    m.w1, m.w3 = m.w13[:, 0:EH], m.w13[:, EH:2 * EH]
    m.w = sb("w", [P, 2 * EH + 2])
    m.w2 = m.w[:, 0:EH].rearrange("p (n c) -> p n c", n=NCH)
    m.wqkv, m.wo = m.w[:, EH:EH + 3 * C], m.w[:, EH + 3 * C:2 * EH]
    m.bqk = m.w[:, 2 * EH:2 * EH + 2]
    m.bias = sb("bias", [P, 2 * C])
    m.bv, m.bo = m.bias[:, 0:C], m.bias[:, C:2 * C]
    m.bqs = sb("bqs", [C, 1])
    m.masks = sb("masks", [P, P + 2 * W], BF16)
    m.identb, m.band, m.bandT = m.masks[:, 0:P], m.masks[:, P:P + W], m.masks[:, P + W:P + 2 * W]
    m.mhalf = sb("mhalf", [P, 1])
    m.zero = sb("zero", [P, 6 * HALF], BF16)
    m.qs_all = sb("qs", [P, NBUF, H, P], BF16)
    m.ks_all = sb("ks", [P, NBUF, H, W], BF16)
    m.qs, m.ks = ([t[:, i] for i in range(NBUF)] for t in (m.qs_all, m.ks_all))

    def sem(name):
        return ctx.enter_context(nc.semaphore(name))

    m.in_x0 = sem("in_x0")
    m.in_x = sem("in_x")
    m.in_small = sem("in_small")
    m.in_w13 = sem("in_w13")
    m.in_w = sem("in_w")
    m.in_masks = sem("in_masks")
    m.in_rows = sem("in_rows")
    m.set = sem("set")
    m.padded = sem("padded")
    m.psum = ctx.enter_context(nc.psum_tensor("psum", [P, 8, 512], F32))
    return m


def ffn_buffers(nc, ctx):
    b = Shared()

    def sb(name, shape, dt=F32):
        return ctx.enter_context(nc.sbuf_tensor(name, shape, dt))

    b.bnst = sb("bnst", [P, R, 6])
    b.mv = sb("mv", [P, R, 2])
    b.ve = sb("ve", [P, R, 1])
    b.nmean = sb("nmean", [P, R, 1])
    b.rstd = sb("rstd", [P, R, 1])
    b.shift = sb("shift", [P, R, 1])
    b.xn = sb("xn", [P, R, C])
    b.xnT = sb("xnT", [C, R, P])
    b.top = sb("top", [P, R, 8])
    b.topi = sb("topi", [P, R, 8], U32)
    b.nmax = sb("nmax", [P, R, 1])
    b.idx = sb("idx", [P, R, 2])
    b.hot1 = sb("hot1", [P, R, E])
    b.hot = sb("hot", [P, R, E])
    b.ex = sb("ex", [P, R, E])
    b.esum = sb("esum", [P, R, 1])
    b.rsum = sb("rsum", [P, R, 1])
    b.sc = sb("sc", [P, R, E])
    b.u = sb("u", [P, 2, EH])
    b.v = sb("v", [P, 2, EH])
    b.uv = sb("uv", [P, 2, EH])
    b.th = sb("th", [P, 2, EH])
    b.h = sb("h", [P, R, EH])
    b.hT = sb("hT", [P, R, NCH, P])
    b.bnst2 = sb("bnst2", [P, R, 6])
    b.mv2 = sb("mv2", [P, R, 2])
    b.ve2 = sb("ve2", [P, R, 1])
    b.nmean2 = sb("nmean2", [P, R, 1])
    b.rstd2 = sb("rstd2", [P, R, 1])
    b.shift2 = sb("shift2", [P, R, 1])
    b.xn2 = sb("xn2", [P, R, C])
    b.xn2T = sb("xn2T", [C, R, P])
    b.qk = sb("qk", [C, R, 2, P])
    b.rest = sb("rest", [C, R, 2, P])
    b.parts = sb("parts", [C, 3, 2, R * P], BF16)
    b.vaug = sb("vaug", [P, R, H, VD])
    return b


def ffn(nc, ctx, m, b, d, which):
    first = which == 0
    X, Y = (m.x[0], m.x[1]) if first else (m.x[2], m.x[3])
    def sem(name):
        return ctx.enter_context(nc.semaphore(f"{name}_{which}"))

    bank = [m.psum[:, i, :] for i in range(8)]
    if first:
        A, B, XT, LG, HT, YP0, YP1, QKV = bank
    else:
        A, B, XT, LG, HT, YP0, YP1 = bank[0], bank[1], bank[6], bank[6][:, 2 * P:], bank[2], bank[3], bank[4]
    YP = (YP0, YP1)

    s = Shared()
    s.bnst = sem("s_bnst")
    s.stats = sem("s_stats")
    s.ve = sem("s_ve")
    s.nmean = sem("s_nmean")
    s.rstd = sem("s_rstd")
    s.shift = sem("s_shift")
    s.xn = sem("s_xn")
    s.xnT_ps = sem("s_xnT_ps")
    s.xnT = sem("s_xnT")
    s.logits = sem("s_logits")
    s.top = sem("s_top")
    s.topi = sem("s_topi")
    s.nmax = sem("s_nmax")
    s.idx = sem("s_idx")
    s.hot1 = sem("s_hot1")
    s.hot = sem("s_hot")
    s.ex = sem("s_ex")
    s.rsum = sem("s_rsum")
    s.sc = sem("s_sc")
    s.a = sem("s_a")
    s.b = sem("s_b")
    s.u = sem("s_u")
    s.v = sem("s_v")
    s.uv = sem("s_uv")
    s.th = sem("s_th")
    s.h = sem("s_h")
    s.hT_ps = sem("s_hT_ps")
    s.hT = sem("s_hT")
    s.y_ps = sem("s_y_ps")
    s.y = sem("s_y")
    s.bnst2 = sem("s_bnst2")
    s.stats2 = sem("s_stats2")
    s.ve2 = sem("s_ve2")
    s.nmean2 = sem("s_nmean2")
    s.rstd2 = sem("s_rstd2")
    s.shift2 = sem("s_shift2")
    s.xn2 = sem("s_xn2")
    s.xn2T_ps = sem("s_xn2T_ps")
    s.xn2T = sem("s_xn2T")
    s.qkv_ps = sem("s_qkv_ps")
    s.qk = sem("s_qk")
    s.part0 = sem("s_part0")
    s.rest = sem("s_rest")
    s.part1 = sem("s_part1")
    s.part2 = sem("s_part2")
    s.vaug = sem("s_vaug")
    s.set = sem("s_set")
    s.free = [sem(f"s_free{i}") for i in range(R // 2)]
    s.out = [sem(f"s_out{i}") for i in range(R)]
    if first:
        RANGE = (-3, NT + 6, 5, 2, R)
    else:
        RANGE = (4, NT + 3, 5, 2, R)

    def ahead(engine, t, part, attention_step):
        at = 3 * (t.at - NT) + part
        if 0 <= at < 2 * PAIRS:
            attention_step(engine, Tile(0, at // PAIRS, NBUF), at % PAIRS)

    def vector_tile(dve, t):
        n, k, k1, k3 = t.n, t.slot, (t + 1).slot, (t + 3).slot
        b1, b3, b5 = (t - 1).slot, (t - 3).slot, (t - 5).slot
        lg = LG[:, 0:E]
        scale = b.sc[:, k, :].unsqueeze(2).broadcast_to([P, E, FH])
        if first and (t + 3).at == 4:
            dve.wait_ge(m.in_x, 16)
        if first and (t + 1).at == 0:
            dve.wait_ge(m.in_small, 16)
        if first and t.at == 1:
            dve.wait_ge(m.in_w, 32)
            nc.vector.tensor_scalar(m.bqs[:], m.bqk[:, 0:1], HD ** -0.5, None, ALU.mult).then_inc(s.set, 1)
        if first:
            ahead(dve, t, 0, s.after.vector_step)
        if (t + 3).exists:
            if not first:
                value = register(dve, n + 4)
                dve.wait_ge(m.in_x0, 16)
                dve.wait_ge(s.before.x2, value)
            nc.vector.bn_stats(b.bnst[:, k3, :], X[:, (t + 3).n, :]).then_inc(s.bnst, 1)
        if (t - 3).exists:
            dve.wait_ge(s.y_ps, n - 2)
            nc.vector.scalar_tensor_tensor(Y[:, (t - 3).n, :], YP[(t - 3).at % 2][:, 0:C], 0.25,
                                           X[:, (t - 3).n, :], ALU.mult, ALU.add).then_inc(s.y, 1)
        if (t + 1).exists:
            value = register(dve, n + 2)
            dve.wait_ge(m.in_x0, 16)
            dve.wait_ge(s.logits, value)
            nc.vector.max(b.top[:, k1, :], lg).then_inc(s.top, 1)
        if (t + 3).exists:
            value = register(dve, n + 4)
            dve.wait_ge(m.in_x0, 16)
            dve.wait_ge(s.bnst, value)
            nc.vector.bn_aggr(b.mv[:, k3, :], b.bnst[:, k3, :]).then_inc(s.stats, 1)
        if (t + 1).exists:
            dve.wait_ge(s.top, n + 2)
            nc.vector.tensor_scalar(b.nmax[:, k1, :], b.top[:, k1, 0:1], -1.0, None, ALU.mult).then_inc(s.nmax, 1)
            nc.vector.max_index(b.topi[:, k1, :], b.top[:, k1, :], lg).then_inc(s.topi, 1)
        if (t + 3).exists:
            dve.wait_ge(s.stats, n + 4)
            nc.vector.tensor_scalar(b.ve[:, k3, :], b.mv[:, k3, 1:2], EPS, None, ALU.add).then_inc(s.ve, 1)
            nc.vector.tensor_scalar(b.nmean[:, k3, :], b.mv[:, k3, 0:1], -1.0, None, ALU.mult
                                    ).then_inc(s.nmean, 1)
        if (t + 1).exists:
            dve.wait_ge(s.topi, n + 2)
            nc.vector.tensor_copy(b.idx[:, k1, :], b.topi[:, k1, 0:2]).then_inc(s.idx, 1)
        if first and (t - 3).exists:
            value = register(dve, n - 2)
            dve.wait_ge(m.in_x0, 16)
            dve.wait_ge(s.y, value)
            nc.vector.bn_stats(b.bnst2[:, b3, :], Y[:, (t - 3).n, :]).then_inc(s.bnst2, 1)
        if t.exists:
            dve.wait_ge(s.a, n + 1)
            dve.wait_ge(s.sc, n + 1)
            nc.vector.tensor_tensor(b.u[:, k % 2, :].rearrange("p (e f) -> p e f", e=E),
                                    A.rearrange("p (e f) -> p e f", e=E), scale, ALU.mult).then_inc(s.u, 1)
        if (t + 1).exists:
            dve.wait_ge(s.idx, n + 2)
            nc.vector.tensor_scalar(b.hot1[:, k1, :], m.iota[:], b.idx[:, k1, 0:1], None,
                                    ALU.is_equal).then_inc(s.hot1, 1)
        if first and (t - 3).exists:
            value = register(dve, n - 2)
            dve.wait_ge(m.in_x0, 16)
            dve.wait_ge(s.bnst2, value)
            nc.vector.bn_aggr(b.mv2[:, b3, :], b.bnst2[:, b3, :]).then_inc(s.stats2, 1)
        if first and (t - 5).exists:
            dve.wait_ge(s.qkv_ps, n - 4)
            dve.wait_ge(s.qk, n - 4)
            dve.wait_ge(s.free[b5 // 2], 16 * NSAVE * (t - 5).round + 16)
            nc.vector.tensor_tensor(b.vaug[:, b5, :, 0:HD],
                                    QKV[:, 2 * P:3 * P].rearrange("p (h d) -> p h d", h=H),
                                    m.bv[:].rearrange("p (h d) -> p h d", h=H), ALU.add).then_inc(s.vaug, 1)
        if first and (t - 3).exists:
            dve.wait_ge(s.stats2, n - 2)
            nc.vector.tensor_scalar(b.ve2[:, b3, :], b.mv2[:, b3, 1:2], EPS, None, ALU.add).then_inc(s.ve2, 1)
            nc.vector.tensor_scalar(b.nmean2[:, b3, :], b.mv2[:, b3, 0:1], -1.0, None, ALU.mult
                                    ).then_inc(s.nmean2, 1)
        if first:
            ahead(dve, t, 1, s.after.vector_step)
        if (t - 1).exists:
            dve.wait_ge(s.th, n)
            dve.wait_ge(s.uv, n)
            nc.vector.scalar_tensor_tensor(b.h[:, b1, :], b.th[:, b1 % 2, :], 1.0, b.uv[:, b1 % 2, :],
                                           ALU.add, ALU.mult).then_inc(s.h, 1)
        if (t + 1).exists:
            dve.wait_ge(s.hot1, n + 2)
            nc.vector.scalar_tensor_tensor(b.hot[:, k1, :], m.iota[:], b.idx[:, k1, 1:2], b.hot1[:, k1, :],
                                           ALU.is_equal, ALU.add).then_inc(s.hot, 1)
            dve.wait_ge(s.ex, n + 2)
            nc.vector.reciprocal(b.rsum[:, k1, :], b.esum[:, k1, :]).then_inc(s.rsum, 1)
        if t.exists:
            dve.wait_ge(s.b, n + 1)
            nc.vector.tensor_tensor(b.v[:, k % 2, :].rearrange("p (e f) -> p e f", e=E),
                                    B.rearrange("p (e f) -> p e f", e=E), scale, ALU.mult).then_inc(s.v, 1)
        if (t + 1).exists:
            dve.wait_ge(s.rsum, n + 2)
            dve.wait_ge(s.hot, n + 2)
            nc.vector.scalar_tensor_tensor(b.sc[:, k1, :], b.ex[:, k1, :], b.rsum[:, k1, :], b.hot[:, k1, :],
                                           ALU.mult, ALU.mult).then_inc(s.sc, 1)

        if first:
            ahead(dve, t, 2, s.after.vector_step)

    def vector(dve):
        if first:
            for i in range(R // 2):
                nc.vector.memset(b.vaug[:, 2 * i:2 * i + 2], 1.0).then_inc(s.free[i], 16)
            dve.wait_ge(m.in_x0, 16)

        run_tiles(dve, *RANGE, vector_tile)

    def gpsimd_tile(pool, t):
        n, k, k3 = t.n, t.slot, (t + 3).slot
        b3, b5 = (t - 3).slot, (t - 5).slot
        if (t + 3).exists:
            pool.wait_ge(s.ve, n + 4)
            nc.gpsimd.tensor_tensor(b.rstd[:, k3, :], b.ve[:, k3, :], m.mhalf[:], ALU.pow).then_inc(s.rstd, 1)
            pool.wait_ge(s.rstd, n + 4)
            pool.wait_ge(s.nmean, n + 4)
            nc.gpsimd.tensor_tensor(b.shift[:, k3, :], b.nmean[:, k3, :], b.rstd[:, k3, :], ALU.mult
                                    ).then_inc(s.shift, 1)
        if first and (t - 5).exists:
            pool.wait_ge(s.part0, n - 4)
            nc.gpsimd.tensor_tensor(b.rest[:, b5], b.qk[:, b5], b.parts[:, 0, :, b5 * P:(b5 + 1) * P], ALU.subtract
                                    ).then_inc(s.rest, 1)
        if first and (t - 3).exists:
            pool.wait_ge(s.ve2, n - 2)
            nc.gpsimd.tensor_tensor(b.rstd2[:, b3, :], b.ve2[:, b3, :], m.mhalf[:], ALU.pow).then_inc(s.rstd2, 1)
            pool.wait_ge(s.rstd2, n - 2)
            pool.wait_ge(s.nmean2, n - 2)
            nc.gpsimd.tensor_tensor(b.shift2[:, b3, :], b.nmean2[:, b3, :], b.rstd2[:, b3, :], ALU.mult
                                    ).then_inc(s.shift2, 1)
        if t.exists:
            pool.wait_ge(s.v, n + 1)
            nc.gpsimd.tensor_tensor(b.uv[:, k % 2, :], b.u[:, k % 2, :], b.v[:, k % 2, :], ALU.mult).then_inc(s.uv, 1)
        if first and (t - 5).exists:
            pool.wait_ge(s.part1, n - 4)
            nc.gpsimd.tensor_tensor(b.parts[:, 2, :, b5 * P:(b5 + 1) * P], b.rest[:, b5],
                                    b.parts[:, 1, :, b5 * P:(b5 + 1) * P], ALU.subtract).then_inc(s.part2, 1)

    def gpsimd(pool):
        run_tiles(pool, -3, *RANGE[1:], gpsimd_tile)

    def scalar_tile(act, t):
        n, k = t.n, t.slot
        if first and t.at == 2:
            act.wait_ge(s.set, 1)
        if first and (t - 5).exists:
            b5 = (t - 5).slot
            act.wait_ge(s.qkv_ps, n - 4)
            nc.scalar.activation(b.qk[:, b5, 0, :], QKV[:, 0:P], ACT.Identity, bias=m.bqs[:], scale=HD ** -0.5)
            nc.scalar.activation(b.qk[:, b5, 1, :], QKV[:, P:2 * P], ACT.Identity,
                                 bias=m.bqk[:, 1:2]).then_inc(s.qk, 1)
        if (t - 2).exists:
            b2 = (t - 2).slot
            act.wait_ge(s.hT_ps, n - 1)
            nc.scalar.activation(b.hT[:, b2].rearrange("p n q -> p (n q)"), HT, ACT.Copy).then_inc(s.hT, 1)
        if first and (t - 4).exists:
            b4 = (t - 4).slot
            act.wait_ge(s.xn2T_ps, n - 3)
            nc.scalar.activation(b.xn2T[:, b4, :], XT[:, P:2 * P], ACT.Copy).then_inc(s.xn2T, 1)
        if (t + 1).exists:
            k1 = (t + 1).slot
            act.wait_ge(s.nmax, n + 2)
            act.wait_ge(s.topi, n + 2)
            nc.scalar.activation(b.ex[:, k1, :], LG[:, 0:E], ACT.Exp, bias=b.nmax[:, k1, :],
                                 accum_out=b.esum[:, k1, :]).then_inc(s.ex, 1)
        if first and (t - 5).exists:
            act.wait_ge(s.qk, n - 4)
            act.wait_ge(s.free[b5 // 2], 16 * NSAVE * (t - 5).round + 16)
            nc.scalar.activation(b.parts[:, 0, :, b5 * P:(b5 + 1) * P], b.qk[:, b5], ACT.Copy).then_inc(s.part0, 1)
        if (t + 2).exists:
            k2 = (t + 2).slot
            act.wait_ge(s.xnT_ps, n + 3)
            nc.scalar.activation(b.xnT[:, k2, :], XT[:, 0:P], ACT.Copy).then_inc(s.xnT, 1)
        if t.exists:
            act.wait_ge(s.u, n + 1)
            nc.scalar.activation(b.th[:, k % 2, :], b.u[:, k % 2, :], ACT.Tanh, scale=0.5).then_inc(s.th, 1)
        if (t + 3).exists:
            k3 = (t + 3).slot
            act.wait_ge(s.shift, n + 4)
            nc.scalar.activation(b.xn[:, k3, :], X[:, (t + 3).n, :], ACT.Identity, bias=b.shift[:, k3, :],
                                 scale=b.rstd[:, k3, :]).then_inc(s.xn, 1)
        if first and t.at == NT + 4:
            s.after.save_maxima(act, Tile(0, 0, NBUF))
        if first and (t - 5).exists:
            act.wait_ge(s.rest, n - 4)
            nc.scalar.activation(b.parts[:, 1, :, b5 * P:(b5 + 1) * P], b.rest[:, b5], ACT.Copy).then_inc(s.part1, 1)
        if first and (t - 3).exists:
            b3 = (t - 3).slot
            act.wait_ge(s.shift2, n - 2)
            nc.scalar.activation(b.xn2[:, b3, :], Y[:, (t - 3).n, :], ACT.Identity, bias=b.shift2[:, b3, :],
                                 scale=b.rstd2[:, b3, :]).then_inc(s.xn2, 1)

    def scalar(act):
        run_tiles(act, *RANGE, scalar_tile)

    def tensor_tile(pe, t):
        n, k = t.n, t.slot
        if first and t.at == 0:
            pe.wait_ge(m.in_w13, 16)
        if first and t.at == 2:
            pe.wait_ge(m.in_w, 32)
        if not first and t.at == -2:
            pe.wait_ge(s.before.nmr, NT)
        if not first and t.at == 0:
            pe.wait_ge(s.before.max, 2 * PAIRS * NT)
        if not first and t.at == 2:
            pe.wait_ge(s.before.exp, PAIRS * NT)
        if not first and t.at == 3:
            pe.wait_ge(s.before.ot, NT)
        if (t - 2).exists:
            b2 = (t - 2).slot
            pe.wait_ge(s.h, n - 1)
            for c in range(NCH):
                last = nc.tensor.transpose(HT[:, c * P:(c + 1) * P], b.h[:, b2, c * P:(c + 1) * P], m.ident[:])
            last.then_inc(s.hT_ps, 1)
        if first:
            ahead(pe, t, 0, s.after.tensor_step)
        if first and (t - 4).exists:
            b4 = (t - 4).slot
            pe.wait_ge(s.xn2, n - 3)
            pe.wait_ge(s.xnT, min(n + 2, NT) if isinstance(n, int) else n + 2)
            nc.tensor.transpose(XT[:, P:2 * P], b.xn2[:, b4, :], m.ident[:]).then_inc(s.xn2T_ps, 1)
        if first:
            ahead(pe, t, 1, s.after.tensor_step)
        if t.exists:
            pe.wait_ge(s.xnT, n + 1)
            pe.wait_ge(s.u, count(n))
            nc.tensor.matmul(A, b.xnT[:, k, :], m.w1[:], start=True, stop=True).then_inc(s.a, 1)
        if t.exists:
            pe.wait_ge(s.v, count(n))
            nc.tensor.matmul(B, b.xnT[:, k, :], m.w3[:], start=True, stop=True).then_inc(s.b, 1)
        if (t + 2).exists:
            pe.wait_ge(s.xn, n + 3)
            pe.wait_ge(s.xnT, count(n + 2))
            if first:
                pe.wait_ge(s.xn2T, count(n - 3))
            else:
                pe.wait_ge(s.topi, count(n + 2))
                pe.wait_ge(s.ex, count(n + 2))
            nc.tensor.transpose(XT[:, 0:P], b.xn[:, (t + 2).slot, :], m.ident[:]).then_inc(s.xnT_ps, 1)
        if (t - 2).exists:
            pe.wait_ge(s.hT, n - 1)
            pe.wait_ge(s.y, count(n - 3))
            for c in range(NCH):
                last = nc.tensor.matmul(YP[t.at % 2][:, 0:C], b.hT[:, b2, c, :], m.w2[:, c, :],
                                        start=(c == 0), stop=(c == NCH - 1))
            last.then_inc(s.y_ps, 1)
        if first:
            ahead(pe, t, 2, s.after.tensor_step)
        if first and (t - 4).exists:
            pe.wait_ge(s.xn2T, n - 3)
            pe.wait_ge(s.vaug, count(n - 4))
            for c in range(2):
                nc.tensor.matmul(QKV[:, c * P:(c + 1) * P], m.wqkv[:, c * C:(c + 1) * C], b.xn2T[:, b4, :],
                                 start=True, stop=True)
            nc.tensor.matmul(QKV[:, 2 * P:3 * P], b.xn2T[:, b4, :], m.wqkv[:, 2 * C:3 * C],
                             start=True, stop=True).then_inc(s.qkv_ps, 1)
        if (t + 2).exists:
            pe.wait_ge(s.xnT, n + 3)
            pe.wait_ge(s.ex, count(n + 2))
            nc.tensor.matmul(LG[:, 0:E], b.xnT[:, (t + 2).slot, :], m.gate[:],
                             start=True, stop=True).then_inc(s.logits, 1)

    def tensor(pe):
        if first:
            pe.wait_ge(m.in_small, 16)

        run_tiles(pe, *RANGE, tensor_tile)

    def sync(sp):
        if first:
            def body(sp, t):
                if t.at == NT - 2 * R:
                    for i in range(R // 2):
                        sp.wait_ge(s.free[i], 16 * NSAVE * (NT // R - 2) + 16)
                    sp.wait_ge(m.padded, 80)
                    for i in range(AHEAD):
                        s.after.load(sp, Tile(0, i, NBUF))
                if t.at % 2 == 0:
                    return
                at, free = (t - 1).n * P, s.free[t.slot // 2]
                sp.wait_ge(s.part2, t.n + 1)
                row = 0
                for kpart, nq in GROUPS:
                    rows = slice(row * HD, (row + nq) * HD)
                    row += nq
                    tiles = slice((t - 1).slot * P, (t.slot + 1) * P)
                    sp.dma_start(d.scrk[rows, :, bass.ds(HALF + at, 2 * P)].rearrange("(p d) h t -> (d h) p t", p=nq),
                                 b.parts[:, kpart, 1, tiles].unsqueeze(1).broadcast_to([C, nq, 2 * P])
                                 ).then_inc(free, 16)
                    sp.dma_start(d.scrq[rows, :, bass.ds(at, 2 * P)].rearrange("(p d) h t -> (d h) p t", p=nq),
                                 b.parts[:, 0:nq, 0, tiles]).then_inc(free, 16)
                sp.wait_ge(s.vaug, t.n + 1)
                sp.dma_start(d.scrv[bass.ds(HALF + at, 2 * P), :].rearrange("(s p) c -> p s c", p=P),
                             b.vaug[:, (t - 1).slot:t.slot + 1].rearrange("p s h d -> p s (h d)")
                             ).then_inc(free, 16)

            run_tiles(sp, 0, NT, 0, NT // R - 2, R, body)
        else:
            def body(sp, t):
                sp.wait_ge(s.y, t.n + 1)
                sp.dma_start(d.out[bass.ds(t.n * P, P), :], Y[:, t.n, :]).then_inc(s.out[t.slot], 16)

            run_tiles(sp, 0, NT, 0, NT // R, R, body)
            for i in range(R):
                sp.wait_ge(s.out[i], 16 * NT // R)

    s.vector, s.gpsimd, s.scalar, s.tensor, s.sync = vector, gpsimd, scalar, tensor, sync
    s.vector_tile, s.scalar_tile, s.tensor_tile = vector_tile, scalar_tile, tensor_tile
    return s


def attention(nc, ctx, m, d, before):
    def sb(name, shape, dt=F32):
        return ctx.enter_context(nc.sbuf_tensor(name, shape, dt))

    def sem(name):
        return ctx.enter_context(nc.semaphore("s_" + name))

    qs, ks = m.qs, m.ks
    vs = [sb(f"vs{i}", [P, 2, H * VD]) for i in range(NBUF)]
    mx = [sb(f"mx{i}", [P, H]) for i in range(NBUF)]
    junk = sb("junk", [P, 4, W], BF16)
    nmr = [sb(f"nmr{i}", [H, P]) for i in range(NBUF)]
    nmp = [sb(f"nmp{i}", [H, 3, P], BF16) for i in range(NBUF)]
    pr = [sb(f"pr{i}", [P, 2, 2, P]) for i in range(4)]
    ot = sb("ot", [P, 4, P])
    rs = sb("rs", [P, H])
    o = sb("o", [P, C])
    oT = sb("oT", [C, P])

    SA = [m.psum[:, i, :] for i in range(2)]
    SB = [m.psum[:, 2 + i, :] for i in range(2)]
    OT, OX, NM, PJ = (m.psum[:, i, :] for i in range(4, 8))

    s = Shared()
    s.max = sem("t_max")
    s.mxT_ps = sem("t_mxT_ps")
    s.nmp0 = sem("t_nmp0")
    s.nmr = sem("t_nmr")
    s.nmp1 = sem("t_nmp1")
    s.nmp2 = sem("t_nmp2")
    s.x1b = sem("t_x1b")
    s.sa = sem("t_sa")
    s.sb = sem("t_sb")
    s.exp = sem("t_exp")
    s.pv = sem("t_pv")
    s.ot = sem("t_ot")
    s.ox = sem("t_ox")
    s.rs = sem("t_rs")
    s.o = sem("t_o")
    s.oT_ps = sem("t_oT_ps")
    s.oT = sem("t_oT")
    s.pj = sem("t_pj")
    s.x2 = sem("t_x2")
    s.q, s.k, s.v, s.nm_in = ([sem(f"t_{name}{i}") for i in range(NBUF)] for name in ("q", "k", "v", "nm_in"))
    RANGE = (2, NT + 4, 4, 3, NBUF)

    def back(t, i, lag):
        return t - (lag - i + PAIRS - 1) // PAIRS, (i - lag) % PAIRS

    def load(sp, t):
        n, k = t.n, t.slot
        sp.wait_ge(s.sb, count(PAIRS * (n - NBUF + 1)))
        sp.dma_start(ks[k][0:R_VALID, :, :], d.scrk[:, :, bass.ds(n * P, W)]).then_inc(s.k[k], 16)
        sp.dma_start(qs[k][0:R_DATA, :, :], d.scrq[:, :, bass.ds(n * P, P)]).then_inc(s.q[k], 16)
        sp.wait_ge(s.pv, count(4 * (n - NBUF + 1)))
        sp.dma_start(vs[k][:], d.scrv[bass.ds(n * P, W), :].rearrange("(s p) c -> p s c", p=P)
                     ).then_inc(s.v[k], 16)

    def save_maxima(queue, t):
        k = t.slot
        for p, part in enumerate((s.nmp0, s.nmp1, s.nmp2)):
            queue.wait_ge(part, t.n + 1)
            queue.dma_start(qs[k][R_VALID + p:R_VALID + p + 1, :, :], nmp[k][:, p, :]
                            ).then_inc(s.nm_in[k], 16)

    s.load, s.save_maxima = load, save_maxima

    def sync(sp):
        def body(sp, t):
            if (t + 1).exists and (t + 1).at >= AHEAD:
                load(sp, t + 1)
            if t.at == 2:
                for i in range(R // 2):
                    sp.wait_ge(before.free[i], 16 * NSAVE * NT // R + 16)
            if (t - 1).exists and (t - 1).at > 0:
                save_maxima(sp, t - 1)

        run_tiles(sp, 0, NT + 1, 3, 3, NBUF, body)

    def gpsimd_tile(pool, t):
        nc.gpsimd.tensor_tensor(m.x1b[:, t.n, :], m.x[1][:, t.n, :], m.bo[:], ALU.add).then_inc(s.x1b, 1)

    def gpsimd(pool):
        pool.wait_ge(m.in_w, 32)
        pool.wait_ge(before.y, NT)
        run_tiles(pool, 0, NT, 0, NT // NBUF, NBUF, gpsimd_tile)

    def vector_step(dve, t, i):
        n, k, j = t.n, t.slot, (t - 1).slot
        if t.exists:
            if t.at == 0 and i == 0:
                dve.wait_ge(m.in_masks, 16)
            value = register(dve, PAIRS * n + i + 1)
            dve.wait_ge(m.in_x0, 16)
            dve.wait_ge(s.sa, value)
            for e in range(2):
                nc.vector.tensor_tensor_reduce(
                    out=junk[:, (2 * i + e) % 4, :], in0=SA[i % 2][:, e * W:(e + 1) * W], in1=m.band[:],
                    scale=1.0, scalar=FLOOR, op0=ALU.add, op1=ALU.max,
                    accum_out=mx[k][:, 2 * i + e:2 * i + e + 1]).then_inc(s.max, 1)
        if i == 1 and (t - 1).exists:
            dve.wait_ge(s.mxT_ps, n)
            dve.wait_ge(s.nm_in[(t - 4).slot], count(48 * (t - 4).round + 48))
            nc.vector.tensor_scalar(nmp[j][:, 0, :], NM[0:H, 0:P], -1.0, None, ALU.mult
                                    ).then_inc(s.nmp0, 1)
        if i == 2 and (t - 1).exists:
            dve.wait_ge(s.nmp0, n)
            nc.vector.scalar_tensor_tensor(nmr[j][:], NM[0:H, 0:P], -1.0, nmp[j][:, 0, :],
                                           ALU.mult, ALU.subtract).then_inc(s.nmr, 1)
        if i == 3 and (t - 1).exists:
            dve.wait_ge(s.nmr, n)
            nc.vector.tensor_copy(nmp[j][:, 1, :], nmr[j][:]).then_inc(s.nmp1, 1)
        if i == 4 and (t - 1).exists:
            dve.wait_ge(s.nmp1, n)
            nc.vector.tensor_tensor(nmp[j][:, 2, :], nmr[j][:], nmp[j][:, 1, :], ALU.subtract
                                    ).then_inc(s.nmp2, 1)
        if i == 4 and (t - 3).exists:
            dve.wait_ge(s.ox, n - 2)
            nc.vector.reciprocal(rs[:].rearrange("p (g j) -> p g j", g=4),
                                 OX.rearrange("p (g j c) -> p g j c", g=4, j=4)[:, :, :, HD]
                                 ).then_inc(s.rs, 1)
        if i == 5 and (t - 3).exists:
            dve.wait_ge(s.rs, n - 2)
            nc.vector.tensor_tensor(o[:].rearrange("p (h d) -> p h d", h=H),
                                    OX.rearrange("p (h c) -> p h c", h=H)[:, :, 0:HD],
                                    rs[:].unsqueeze(2).broadcast_to([P, H, HD]), ALU.mult
                                    ).then_inc(s.o, 1)
        if i == 0 and (t - 4).exists:
            dve.wait_ge(s.pj, n - 3)
            dve.wait_ge(s.x1b, n - 3)
            nc.vector.tensor_tensor(m.x[2][:, (t - 4).n, :], PJ[:, P:P + C], m.x1b[:, (t - 4).n, :],
                                    ALU.add).then_inc(s.x2, 1)

    def vector_tile(dve, t):
        for i in range(PAIRS):
            vector_step(dve, t, i)
            if (t.at, i) in BETWEEN:
                s.after.vector_tile(dve, Tile(0, BETWEEN[t.at, i], R))

    def vector(dve):
        run_tiles(dve, *RANGE, vector_tile)

    def scalar_step(act, t, i):
        if i == 2 and (t - 3).exists:
            act.wait_ge(s.pv, 4 * (t - 2).n)
            nc.scalar.activation(ot[:].rearrange("p g q -> p (g q)"), OT, ACT.Copy).then_inc(s.ot, 1)
        if i == 7 and (t - 3).exists:
            act.wait_ge(s.oT_ps, (t - 2).n)
            nc.scalar.activation(oT[:], PJ[:, 0:P], ACT.Copy).then_inc(s.oT, 1)
        tb, pb = back(t, i, LAG)
        if tb.exists:
            act.wait_ge(s.sb, PAIRS * tb.n + pb + 1)
            act.wait_ge(s.pv, count(4 * tb.n + pb // 2 - 1))
            nc.scalar.activation(pr[pb % 4][:].rearrange("p h s q -> p (h s q)"), SB[pb % 2],
                                 ACT.Exp).then_inc(s.exp, 1)

    def scalar_tile(act, t):
        for i in range(PAIRS):
            scalar_step(act, t, i)
            if (t.at, i) in BETWEEN:
                s.after.scalar_tile(act, Tile(0, BETWEEN[t.at, i], R))

    def scalar(act):
        run_tiles(act, *RANGE, scalar_tile)

    def tensor_step(pe, t, i):
        n, k = t.n, t.slot
        if t.exists:
            if t.at == 0 and i == 0:
                pe.wait_ge(m.in_masks, 16)
                pe.wait_ge(m.in_rows, 64)
                pe.wait_ge(before.u, NT)
                pe.wait_ge(before.v, NT)
            if i == 0:
                pe.wait_ge(s.q[k], 16 * (t.round + 1))
                pe.wait_ge(s.k[k], 16 * (t.round + 1))
            pe.wait_ge(s.max, count(2 * (PAIRS * n + i - 1)))
            for e in range(2):
                last = nc.tensor.matmul(SA[i % 2][:, e * W:(e + 1) * W], qs[k][0:R_VALID, 2 * i + e, :],
                                        ks[k][0:R_VALID, 2 * i + e, :], start=True, stop=True)
            last.then_inc(s.sa, 1)
        if i == 1 and (t - 1).exists:
            if t.at == 1:
                pe.wait_ge(before.y, NT)
            pe.wait_ge(s.max, 2 * PAIRS * n)
            pe.wait_ge(s.nmr, count(n - 1))
            nc.tensor.transpose(NM[0:H, 0:P], mx[(t - 1).slot][:], m.ident[:]).then_inc(s.mxT_ps, 1)
        tb, pb = back(t, i, LAG)
        if tb.exists:
            kb = tb.slot
            if pb == 0:
                pe.wait_ge(s.nm_in[kb], 48 * (tb.round + 1))
            pe.wait_ge(s.exp, count(PAIRS * tb.n + pb - 1))
            bank = SB[pb % 2]
            nc.tensor.matmul(bank.rearrange("p (h k) -> p h k", h=2), m.identb[:],
                             m.bandT[:].unsqueeze(1).broadcast_to([P, 2, W]), start=True, stop=False)
            for e in range(2):
                for half in range(2):
                    at = (2 * e + half) * P
                    last = nc.tensor.matmul(bank[:, at:at + P],
                                            ks[kb][:, 2 * pb + e, half * P:(half + 1) * P],
                                            qs[kb][:, 2 * pb + e, :], start=False,
                                            stop=(e == 1 and half == 1))
            last.then_inc(s.sb, 1)
        tv, pv = back(t, i, LAG + 2)
        if pv % 2 == 1 and tv.exists:
            kv, g = tv.slot, pv // 2
            pe.wait_ge(s.exp, PAIRS * tv.n + pv + 1)
            if g == 0:
                pe.wait_ge(s.v[kv], 16 * (tv.round + 1))
                pe.wait_ge(s.ot, count(tv.n))
            for half in range(2):
                for j in range(4):
                    hh = 4 * g + j
                    last = nc.tensor.matmul(OT[32 * j:32 * j + VD, g * P:(g + 1) * P],
                                            vs[kv][:, half, hh * VD:(hh + 1) * VD],
                                            pr[(2 * g + j // 2) % 4][:, j % 2, half, :],
                                            start=(half == 0), stop=(half == 1))
            last.then_inc(s.pv, 1)
        if i == 3 and (t - 3).exists:
            pe.wait_ge(s.ot, n - 2)
            pe.wait_ge(s.o, n - 3)
            for g in range(4):
                last = nc.tensor.transpose(OX[:, g * P:(g + 1) * P], ot[:, g, :], m.ident[:])
            last.then_inc(s.ox, 1)
        if i == 6 and (t - 3).exists:
            pe.wait_ge(s.o, n - 2)
            pe.wait_ge(s.x2, n - 3)
            nc.tensor.transpose(PJ[:, 0:P], o[:], m.ident[:]).then_inc(s.oT_ps, 1)
        if i == 7 and (t - 3).exists:
            pe.wait_ge(s.oT, n - 2)
            nc.tensor.matmul(PJ[:, P:P + C], oT[:], m.wo[:], start=True, stop=True).then_inc(s.pj, 1)

    def tensor_tile(pe, t):
        for i in range(PAIRS):
            tensor_step(pe, t, i)
            if (t.at, i) in BETWEEN:
                s.after.tensor_tile(pe, Tile(0, BETWEEN[t.at, i], R))

    def tensor(pe):
        pe.wait_ge(before.xn2T, NT)
        pe.wait_ge(before.topi, NT)
        pe.wait_ge(before.ex, NT)
        pe.wait_ge(before.hT, NT)
        pe.wait_ge(before.y, NT)
        pe.wait_ge(before.qk, NT)
        pe.wait_ge(before.vaug, NT)

        run_tiles(pe, *RANGE, tensor_tile)

    s.vector, s.gpsimd, s.scalar, s.tensor, s.sync = vector, gpsimd, scalar, tensor, sync
    s.vector_step, s.tensor_step = vector_step, tensor_step
    return s


def load(sp, m, d):
    xv = d.x.rearrange("(t p) c -> p t c", p=P)
    sp.dma_start(m.x[0][:, 0:4, :], xv[:, 0:4, :]).then_inc(m.in_x0, 16)
    sp.dma_start(m.small[:], d.small).then_inc(m.in_small, 16)
    sp.dma_start(m.w13[:], d.w13).then_inc(m.in_w13, 16)
    sp.dma_start(m.x[0][:, 4:NT, :], xv[:, 4:NT, :]).then_inc(m.in_x, 16)
    sp.dma_start(m.w[:], d.w).then_inc(m.in_w, 16)
    sp.dma_start(m.bias[:], d.bias.partition_broadcast(P)).then_inc(m.in_w, 16)
    sp.dma_start(m.masks[:], d.masks).then_inc(m.in_masks, 16)
    for dst, rows, src in ((m.qs_all, slice(R_DATA, R_VALID), d.ones), (m.ks_all, slice(R_VALID, R_ALL), d.ones),
                           (m.qs_all, slice(R_ALL, P), d.zeros), (m.ks_all, slice(R_ALL, P), d.zeros)):
        size = dst.shape[1] * dst.shape[2] * dst.shape[3]
        sp.dma_start(dst[rows].rearrange("r n h q -> r (n h q)"),
                     src[0:size].partition_broadcast(rows.stop - rows.start)).then_inc(m.in_rows, 16)
    sp.wait_ge(m.set, 2)
    for at in (0, T + HALF):
        sp.dma_start(d.scrk[0:R_DATA, :, at:at + HALF].rearrange("r h t -> (r h) t")
                     .rearrange("(p k) t -> p k t", k=6),
                     m.zero[:, :].rearrange("p (k t) -> p k t", k=6)).then_inc(m.padded, 16)
        sp.dma_start(d.scrv[at:at + HALF, :],
                     m.zero[0:HALF, 0:2 * H * VD].bitcast(F32)).then_inc(m.padded, 16)
    sp.dma_start(d.scrk[R_DATA:R_VALID, :, :], d.valid).then_inc(m.padded, 16)


def build(nc, d):
    with ExitStack() as ctx:
        m = allocate(nc, ctx)
        b = ffn_buffers(nc, ctx)
        first = ffn(nc, ctx, m, b, d, 0)
        att = attention(nc, ctx, m, d, first)
        second = ffn(nc, ctx, m, b, d, 1)
        first.after, att.after, second.before = att, second, att
        block = ctx.enter_context(nc.Block())

        @block.sync
        def _(sp):
            load(sp, m, d)
            first.sync(sp)
            att.sync(sp)
            second.sync(sp)

        @block.gpsimd
        def _(pool):
            pool.wait_ge(m.set, 2)
            first.gpsimd(pool)
            att.gpsimd(pool)
            second.gpsimd(pool)

        @block.vector
        def _(dve):
            nc.vector.memset(m.zero[:], 0.0).then_inc(m.set, 1)
            nc.vector.memset(m.mhalf[:], -0.5).then_inc(m.set, 1)
            first.vector(dve)
            att.vector(dve)
            second.vector(dve)

        @block.scalar
        def _(act):
            first.scalar(act)
            att.scalar(act)
            second.scalar(act)

        @block.tensor
        def _(pe):
            first.tensor(pe)
            att.tensor(pe)
            second.tensor(pe)


def kernel(L0_attn_x, L0_attn_in_proj_w, L0_attn_in_proj_b, L0_attn_out_w, L0_attn_out_b, L0_ffn_gate_w, L0_ffn_w1,
           L0_ffn_w2, L0_ffn_w3):
    import concourse.bacc as _bacc
    import ml_dtypes
    from concourse.bass_utils import run_bass_kernel_spmd as _run

    def flat(a):
        return np.ascontiguousarray(a)

    i, c = np.arange(P)[:, None], np.arange(W)[None, :]
    band = np.where((c >= i) & (c <= i + 2 * HALF), 0.0, BIG).astype(ml_dtypes.bfloat16)
    q = c % P
    bandT = np.where(np.where(c < P, q <= i, q >= i), 0.0, BIG).astype(ml_dtypes.bfloat16)
    exists = np.full((1, H, TP), BIG)
    exists[:, :, HALF:HALF + T] = 0.0
    w1, w3 = (np.transpose(w, (1, 0, 2)).reshape(C, EH) for w in (L0_ffn_w1, L0_ffn_w3))
    w2 = np.transpose(np.reshape(L0_ffn_w2, (NCH, P, C)), (1, 0, 2)).reshape(P, EH)
    wqk = np.transpose(np.reshape(L0_attn_in_proj_w[0:2 * C], (2, H, HD, C)), (3, 0, 2, 1)).reshape(C, 2 * C)
    wv, wo = np.transpose(L0_attn_in_proj_w[2 * C:]), np.transpose(L0_attn_out_w)
    bqk = np.transpose(np.reshape(L0_attn_in_proj_b[0:2 * C], (2, H, HD)), (2, 1, 0)).reshape(C, 2)
    iota = np.broadcast_to(np.arange(E, dtype=np.float32), (P, E))
    arrays = {
        "x": flat(L0_attn_x).reshape(T, C),
        "small": np.concatenate([L0_ffn_gate_w, iota, np.eye(P, dtype=np.float32)], axis=1),
        "w13": np.concatenate([w1, w3], axis=1),
        "w": np.concatenate([w2, wqk, wv, wo, bqk], axis=1),
        "bias": np.concatenate([L0_attn_in_proj_b[2 * C:], L0_attn_out_b]),
        "masks": np.concatenate([np.eye(P).astype(ml_dtypes.bfloat16), band, bandT], axis=1),
        "valid": exists.astype(ml_dtypes.bfloat16),
        "ones": np.ones(NBUF * H * W, ml_dtypes.bfloat16),
        "zeros": np.zeros(NBUF * H * W, ml_dtypes.bfloat16),
    }
    nc = _bacc.Bacc("TRN2", target_bir_lowering=False, num_devices=1)

    def dram(name):
        a = arrays[name]
        return nc.dram_tensor(f"in_{name}", a.shape, mybir.dt.from_np(a.dtype), kind="ExternalInput").ap()

    d = Shared()
    d.x = dram("x")
    d.small = dram("small")
    d.w13 = dram("w13")
    d.w = dram("w")
    d.bias = dram("bias")
    d.masks = dram("masks")
    d.valid = dram("valid")
    d.ones = dram("ones")
    d.zeros = dram("zeros")
    d.scrk = nc.dram_tensor("scrk", (R_VALID, H, TP), BF16, kind="Internal").ap()
    d.scrq = nc.dram_tensor("scrq", (R_DATA, H, T), BF16, kind="Internal").ap()
    d.scrv = nc.dram_tensor("scrv", (TP, H * VD), F32, kind="Internal").ap()
    d.out = nc.dram_tensor("out_0", (T, C), F32, kind="ExternalOutput").ap()
    build(nc, d)
    r = _run(nc, [{f"in_{name}": a for name, a in arrays.items()}], core_ids=[0])
    return r.results[0]["out_0"].reshape(1, T, C)
```
